# Optimizing a Trainium2 kernel written in Bass

```python
import numpy as np
import jax
import jax.numpy as jnp

def _softmax(x, axis=-1):
    return jax.nn.softmax(x, axis=axis)

def _gelu(x):
    return jax.nn.gelu(x, approximate=True)

def _silu(x):
    return jax.nn.silu(x)

def _sigmoid(x):
    return jax.nn.sigmoid(x)

def _layernorm(x, axis=-1, eps=1e-05):
    m = jnp.mean(x, axis=axis, keepdims=True)
    v = jnp.var(x, axis=axis, keepdims=True)
    return (x - m) / jnp.sqrt(v + eps)

def _scatter_add(tgt, idx, src, axis=0):
    return tgt.at[idx].add(src)

def _segment_sum(src, seg, n):
    return jax.ops.segment_sum(src, seg, n)
kernel_name = 'mk_gnn_ffn_d2_gnn_r8_bfcf9a'

def setup_inputs(seed: int=0):
    np.random.seed(seed)
    _w = jnp.asarray

    def _rec_inputs():
        import jax
        import jax.numpy as jnp
        _gk = jax.random.key(seed)
        x = -0.0003713 + 1 * jax.random.normal(jax.random.fold_in(_gk, 1), (6250, 256), jnp.float32)
        _s = jax.random.randint(jax.random.fold_in(_gk, 2), (50000,), 0, 6250, jnp.int32)
        _d = jax.random.randint(jax.random.fold_in(_gk, 3), (50000,), 0, 6250, jnp.int32)
        _loop = jnp.arange(6250, dtype=jnp.int32)
        src = jnp.concatenate([_s, _d, _loop])
        dst = jnp.concatenate([_d, _s, _loop])
        _o = jnp.argsort(dst, stable=True)
        src = src[_o]
        dst = dst[_o]
        return (x, src, dst)
    x, src, dst = _rec_inputs()

    def _L0_gnn_setup():
        import jax, jax.numpy as jnp
        import numpy as np
        N_NODES = 6250
        N_EDGES = 100000
        IN_DIM = 256
        OUT_DIM = 64
        HEADS = 4
        NEG_SLOPE = 0.2
        key = jax.random.key(seed)
        k1, k2, k3, k4, k5, k6 = jax.random.split(key, 6)
        x = jax.random.normal(k1, (N_NODES, IN_DIM), dtype=jnp.float32)
        edge_index = jax.random.randint(k2, (2, N_EDGES), 0, N_NODES, dtype=jnp.int64)
        scale = 1.0 / np.sqrt(IN_DIM)
        W = jax.random.normal(k3, (IN_DIM, HEADS * OUT_DIM), dtype=jnp.float32) * scale
        att_src = jax.random.normal(k4, (HEADS, OUT_DIM), dtype=jnp.float32) * scale
        att_dst = jax.random.normal(k5, (HEADS, OUT_DIM), dtype=jnp.float32) * scale
        bias = jnp.zeros((HEADS * OUT_DIM,), dtype=jnp.float32)
        return {'x': x, 'edge_index': edge_index, 'W': W, 'att_src': att_src, 'att_dst': att_dst, 'bias': bias}
    _L0_gnn_all = _L0_gnn_setup()
    _L0_gnn_in = {k: v for k, v in _L0_gnn_all.items() if k in ('W', 'att_src', 'att_dst', 'bias')}
    del _L0_gnn_all

    def _L0_ffn_setup():
        import jax, jax.numpy as jnp
        import numpy as np
        E = 8
        K = 2
        D = 256
        H = 512
        DOUT = 256
        EPS = 1e-05
        key = jax.random.key(seed)
        ks = jax.random.split(key, 9)
        s = 0.02
        return {'x': jax.random.normal(ks[0], (4, 1024, D), jnp.float32), 'gamma': 1.0 + 0.05 * jax.random.normal(ks[1], (D,), jnp.float32), 'beta': 0.05 * jax.random.normal(ks[2], (D,), jnp.float32), 'Wr': 0.01 * jax.random.normal(ks[3], (D, E), jnp.float32), 'br': jnp.zeros((E,), jnp.float32), 'W1': s * jax.random.normal(ks[4], (E, D, H), jnp.float32), 'b1': s * jax.random.normal(ks[5], (E, H), jnp.float32), 'W2': s * jax.random.normal(ks[6], (E, H, DOUT), jnp.float32), 'b2': s * jax.random.normal(ks[7], (E, DOUT), jnp.float32)}
    _L0_ffn_all = _L0_ffn_setup()
    _L0_ffn_in = {k: v for k, v in _L0_ffn_all.items() if k in ('gamma', 'beta', 'Wr', 'br', 'W1', 'b1', 'W2', 'b2')}
    del _L0_ffn_all

    def _L1_gnn_setup():
        import jax, jax.numpy as jnp
        import numpy as np
        N_NODES = 6250
        N_EDGES = 100000
        IN_CH = 256
        HID_CH = 256
        OUT_CH = 256
        N_LAYERS = 3
        key = jax.random.key(seed)
        ks = jax.random.split(key, 8)
        s_in = 1.0 / np.sqrt(IN_CH)
        s_h = 1.0 / np.sqrt(HID_CH)
        return {'x': jax.random.normal(ks[0], (N_NODES, IN_CH), dtype=jnp.float32), 'W_in': jax.random.normal(ks[1], (IN_CH, HID_CH), dtype=jnp.float32) * s_in, 'b_in': jnp.zeros((HID_CH,), dtype=jnp.float32), 'W_agg': jax.random.normal(ks[2], (N_LAYERS, HID_CH, HID_CH), dtype=jnp.float32) * s_h, 'W_self': jax.random.normal(ks[3], (N_LAYERS, HID_CH, HID_CH), dtype=jnp.float32) * s_h, 'b_hid': jnp.zeros((N_LAYERS, HID_CH), dtype=jnp.float32), 'W_out': jax.random.normal(ks[4], (HID_CH, OUT_CH), dtype=jnp.float32) * s_h, 'b_out': jnp.zeros((OUT_CH,), dtype=jnp.float32), 'edge_index': jax.random.randint(ks[5], (2, N_EDGES), 0, N_NODES, dtype=jnp.int64)}
    _L1_gnn_all = _L1_gnn_setup()
    _L1_gnn_in = {k: v for k, v in _L1_gnn_all.items() if k in ('W_in', 'b_in', 'W_agg', 'W_self', 'b_hid', 'W_out', 'b_out')}
    del _L1_gnn_all

    def _L1_ffn_setup():
        import math
        import jax, jax.numpy as jnp
        import numpy as np
        CAPACITY_FACTOR = 1.25
        key = jax.random.key(seed)
        ks = jax.random.split(key, 5)
        B, L, D, F, E = (8, 1024, 256, 1024, 8)
        h = jax.random.normal(ks[0], (B, L, D), dtype=jnp.float32)
        gate_w = jax.random.normal(ks[1], (D, E), dtype=jnp.float32) * 0.02
        gate_b = jnp.zeros((E,), dtype=jnp.float32)
        w1 = jax.random.normal(ks[2], (E, D, F), dtype=jnp.float32) * (1.0 / math.sqrt(D))
        b1 = jnp.zeros((E, F), dtype=jnp.float32)
        w2 = jax.random.normal(ks[3], (E, F, D), dtype=jnp.float32) * (1.0 / math.sqrt(F))
        b2 = jnp.zeros((E, D), dtype=jnp.float32)
        return {'h': h, 'gate_w': gate_w, 'gate_b': gate_b, 'w1': w1, 'b1': b1, 'w2': w2, 'b2': b2}
    _L1_ffn_all = _L1_ffn_setup()
    _L1_ffn_in = {k: v for k, v in _L1_ffn_all.items() if k in ('gate_w', 'gate_b', 'w1', 'b1', 'w2', 'b2')}
    del _L1_ffn_all
    return {'x': x, 'src': src, 'dst': dst, 'L0_gnn_W': _L0_gnn_in['W'], 'L0_gnn_att_src': _L0_gnn_in['att_src'], 'L0_gnn_att_dst': _L0_gnn_in['att_dst'], 'L0_gnn_bias': _L0_gnn_in['bias'], 'L0_ffn_gamma': _L0_ffn_in['gamma'], 'L0_ffn_beta': _L0_ffn_in['beta'], 'L0_ffn_Wr': _L0_ffn_in['Wr'], 'L0_ffn_br': _L0_ffn_in['br'], 'L0_ffn_W1': _L0_ffn_in['W1'], 'L0_ffn_b1': _L0_ffn_in['b1'], 'L0_ffn_W2': _L0_ffn_in['W2'], 'L0_ffn_b2': _L0_ffn_in['b2'], 'L1_gnn_W_in': _L1_gnn_in['W_in'], 'L1_gnn_b_in': _L1_gnn_in['b_in'], 'L1_gnn_W_agg': _L1_gnn_in['W_agg'], 'L1_gnn_W_self': _L1_gnn_in['W_self'], 'L1_gnn_b_hid': _L1_gnn_in['b_hid'], 'L1_gnn_W_out': _L1_gnn_in['W_out'], 'L1_gnn_b_out': _L1_gnn_in['b_out'], 'L1_ffn_gate_w': _L1_ffn_in['gate_w'], 'L1_ffn_gate_b': _L1_ffn_in['gate_b'], 'L1_ffn_w1': _L1_ffn_in['w1'], 'L1_ffn_b1': _L1_ffn_in['b1'], 'L1_ffn_w2': _L1_ffn_in['w2'], 'L1_ffn_b2': _L1_ffn_in['b2']}

def reference(x, src, dst, L0_gnn_W, L0_gnn_att_src, L0_gnn_att_dst, L0_gnn_bias, L0_ffn_gamma, L0_ffn_beta, L0_ffn_Wr, L0_ffn_br, L0_ffn_W1, L0_ffn_b1, L0_ffn_W2, L0_ffn_b2, L1_gnn_W_in, L1_gnn_b_in, L1_gnn_W_agg, L1_gnn_W_self, L1_gnn_b_hid, L1_gnn_W_out, L1_gnn_b_out, L1_ffn_gate_w, L1_ffn_gate_b, L1_ffn_w1, L1_ffn_b1, L1_ffn_w2, L1_ffn_b2):
    import jax
    import jax.numpy as jnp

    def _L0_gnn_ref(x, edge_index, W, att_src, att_dst, bias):
        import jax, jax.numpy as jnp
        import numpy as np
        N_NODES = 6250
        N_EDGES = 100000
        IN_DIM = 256
        OUT_DIM = 64
        HEADS = 4
        NEG_SLOPE = 0.2
        N = x.shape[0]
        H, C = att_src.shape
        loop = jnp.arange(N, dtype=edge_index.dtype)
        src = jnp.concatenate([edge_index[0], loop])
        dst = jnp.concatenate([edge_index[1], loop])
        h = (x @ W).reshape(N, H, C)
        a_src = jnp.einsum('nhc,hc->nh', h, att_src)
        a_dst = jnp.einsum('nhc,hc->nh', h, att_dst)
        e = jax.nn.leaky_relu(a_src[src] + a_dst[dst], negative_slope=NEG_SLOPE)
        m = jax.ops.segment_max(e, dst, num_segments=N)
        p = jnp.exp(e - m[dst])
        denom = jax.ops.segment_sum(p, dst, num_segments=N)
        alpha = p / (denom[dst] + 1e-16)
        out = jax.ops.segment_sum(alpha[:, :, None] * h[src], dst, num_segments=N)
        out = out.reshape(N, H * C) + bias
        return jax.nn.relu(out)

    def _L0_ffn_ref(x, gamma, beta, Wr, br, W1, b1, W2, b2):
        import jax, jax.numpy as jnp
        import numpy as np
        E = 8
        K = 2
        D = 256
        H = 512
        DOUT = 256
        EPS = 1e-05
        mu = jnp.mean(x, axis=-1, keepdims=True)
        var = jnp.mean(jnp.square(x - mu), axis=-1, keepdims=True)
        xn = (x - mu) * jax.lax.rsqrt(var + EPS) * gamma + beta
        logits = jnp.einsum('bsd,de->bse', xn, Wr) + br
        top_vals, top_idx = jax.lax.top_k(logits, K)
        w = jax.nn.softmax(top_vals, axis=-1)
        w_full = jnp.einsum('bsk,bske->bse', w, jax.nn.one_hot(top_idx, E, dtype=w.dtype))
        y = jnp.zeros(x.shape[:-1] + (DOUT,), x.dtype)
        for e in range(E):
            h = jax.nn.gelu(jnp.einsum('bsd,dh->bsh', xn, W1[e]) + b1[e], approximate=False)
            y_e = jnp.einsum('bsh,hd->bsd', h, W2[e]) + b2[e]
            y = y + y_e * w_full[..., e, None]
        return y

    def _L1_gnn_ref(x, W_in, b_in, W_agg, W_self, b_hid, W_out, b_out, edge_index):
        import jax, jax.numpy as jnp
        import numpy as np
        N_NODES = 6250
        N_EDGES = 100000
        IN_CH = 256
        HID_CH = 256
        OUT_CH = 256
        N_LAYERS = 3
        n = x.shape[0]
        dst = edge_index[0]
        src = edge_index[1]
        n_layers = W_agg.shape[0]
        h = x @ W_in + b_in
        deg = jax.ops.segment_sum(jnp.ones_like(dst, dtype=h.dtype), dst, num_segments=n)
        deg = jnp.maximum(deg, 1.0)[:, None]
        for l in range(n_layers):
            agg = jax.ops.segment_sum(h[src], dst, num_segments=n) / deg
            h = jax.nn.relu(agg @ W_agg[l] + h @ W_self[l] + b_hid[l])
        return h @ W_out + b_out

    def _L1_ffn_ref(h, gate_w, gate_b, w1, b1, w2, b2):
        import math
        import jax, jax.numpy as jnp
        import numpy as np
        CAPACITY_FACTOR = 1.25
        B, L, D = h.shape
        E = gate_w.shape[1]
        T = B * L
        C = max(1, math.ceil(CAPACITY_FACTOR * T / E))
        x = h.reshape(T, D)
        logits = x @ gate_w + gate_b
        probs = jax.nn.softmax(logits, axis=-1)
        idx = jnp.argmax(probs, axis=-1)
        prb = jnp.take_along_axis(probs, idx[:, None], axis=1)[:, 0]
        one_hot = jax.nn.one_hot(idx, E, dtype=jnp.float32)
        pos = (jnp.cumsum(one_hot, axis=0) * one_hot).sum(-1).astype(jnp.int32) - 1
        kept = pos < C
        pos_safe = jnp.where(kept, pos, C)
        buf = jnp.zeros((E, C, D), dtype=h.dtype).at[idx, pos_safe].set(x, mode='drop')
        hmid = jax.nn.relu(jnp.einsum('ecd,edf->ecf', buf, w1) + b1[:, None, :])
        ybuf = jnp.einsum('ecf,efd->ecd', hmid, w2) + b2[:, None, :]
        pos_g = jnp.minimum(pos, C - 1)
        y_tok = ybuf[idx, pos_g] * (prb * kept)[:, None]
        y = y_tok.reshape(B, L, D)
        y = jnp.nan_to_num(y, nan=0.0, posinf=10000.0, neginf=-10000.0)
        return y
    edge_index = jnp.stack([src, dst])
    x = x + _L0_gnn_ref(_layernorm(x, axis=-1), edge_index, L0_gnn_W, L0_gnn_att_src, L0_gnn_att_dst, L0_gnn_bias)
    x = x + _L0_ffn_ref(_layernorm(x, axis=-1)[None], L0_ffn_gamma, L0_ffn_beta, L0_ffn_Wr, L0_ffn_br, L0_ffn_W1, L0_ffn_b1, L0_ffn_W2, L0_ffn_b2)[0]
    x = x + _L1_gnn_ref(_layernorm(x, axis=-1), L1_gnn_W_in, L1_gnn_b_in, L1_gnn_W_agg, L1_gnn_W_self, L1_gnn_b_hid, L1_gnn_W_out, L1_gnn_b_out, edge_index)
    x = x + _L1_ffn_ref(_layernorm(x, axis=-1)[None], L1_ffn_gate_w, L1_ffn_gate_b, L1_ffn_w1, L1_ffn_b1, L1_ffn_w2, L1_ffn_b2)[0]
    return x

_drawn_inputs = setup_inputs


def setup_inputs(seed=0):
    import zlib

    import numpy as np

    out = dict(_drawn_inputs(seed))
    spreads = {'L0_gnn_bias': (0.0, 0.1),
     'L0_ffn_br': (0.0, 0.1),
     'L1_gnn_b_in': (0.0, 0.1),
     'L1_gnn_b_hid': (0.0, 0.1),
     'L1_gnn_b_out': (0.0, 0.1),
     'L1_ffn_gate_b': (0.0, 0.1),
     'L1_ffn_b1': (0.0, 0.725),
     'L1_ffn_b2': (0.0, 0.508)}
    factors = {'L0_ffn_gamma': 4.786, 'L0_ffn_beta': 4.15, 'L0_ffn_b1': 6.302, 'L0_ffn_b2': 2.889}
    for name, (base, spread) in spreads.items():
        noise = np.random.default_rng([zlib.crc32(name.encode()), seed]).standard_normal(out[name].shape)
        drawn = base * np.exp(spread * noise) if base else spread * noise
        out[name] = jnp.asarray(drawn.astype(out[name].dtype))
    for name, factor in factors.items():
        out[name] = (out[name] * factor).astype(out[name].dtype)
    return out
```

```python
import numpy as np
import concourse.bass as bass
from concourse import mybir
from contextlib import ExitStack

F32 = mybir.dt.float32
BF16 = mybir.dt.bfloat16
I32 = mybir.dt.int32
U32 = mybir.dt.uint32
ALU = mybir.AluOpType
ACT = mybir.ActivationFunctionType
AX = mybir.AxisListType

P = 128
N = 6250
D = 256
KD = D // P
NT = -(-N // P)
NP = NT * P
LAST = N - (NT - 1) * P
E = 106250
EP, EC = 125, 850
U, R = 4, 4
AHEAD = 3
STEP = U * R
C = -(-((E + NT * (P - 1)) // P) // STEP) * STEP
HEADS, HD = 4, D // 4
SLOPE = 0.2
EPS = 1e-5
BIG = 2.0 ** 120
G = 7
NG = NT // G
NE = 8
F0 = 512
F1 = 1024
CAP = -(-N * 5 // (4 * NE))
SLOTS = -(-CAP // P) * P
ST = SLOTS // P
SC = 5


def each(engine, body, n):
    body(0, True)
    with engine.Fori(1, n) as i:
        body(i, False)


class Ctx:

    def __init__(self, nc, inputs, out):
        self.nc, self.inp, self.out = nc, inputs, out


class Stage(ExitStack):

    def __init__(self, nc):
        super().__init__()
        self.nc, self.used = nc, []

    def semaphore(self, name):
        self.used.append(self.nc.alloc_semaphore(name))
        return self.used[-1]

    def __exit__(self, *how):
        super().__exit__(*how)
        if how[0] is None:
            self.nc.clear_and_free_semaphores(self.used)
            self.nc.all_engine_barrier()


def sems(nc, stage, prefix, names):
    return [stage.semaphore(f"{prefix}_{n}") for n in names.split()]


def setup(g):
    nc = g.nc
    with Stage(g.nc) as s:
        loaded, built, zeroed, filled, fill_ready = sems(nc, s, "set", "loaded built zeroed filled fill_ready")
        fill = s.enter_context(nc.sbuf_tensor("fill", [P, C, 2], I32))
        block = s.enter_context(nc.Block())

        @block.sync
        def _(sp):
            x = g.inp["x"]
            sp.dma_start(g.X[:, 0:NT - 1, :], x[0:(NT - 1) * P, :].rearrange("(t p) d -> p t d", p=P)).then_inc(loaded, 16)
            sp.wait_ge(zeroed, 1)
            sp.dma_start(g.X[0:LAST, NT - 1, :], x[(NT - 1) * P:N, :]).then_inc(loaded, 16)
            sp.wait_ge(fill_ready, 1)
            for rec in g.records:
                sp.dma_start(rec, fill[:, :, :]).then_inc(filled, 16)
            sp.wait_ge(filled, 32)
            sp.wait_ge(loaded, 32)

        @block.vector
        def _(dve):
            dve.memset(g.X[:, NT - 1, :], 0.0).then_inc(zeroed, 1)
            dve.memset(g.ones[:, :], 1.0)
            dve.memset(g.ident[:, :], 0.0).then_inc(built, 1)
            dve.memset(fill[:, :, 0], 0)
            dve.memset(fill[:, :, 1], -1).then_inc(fill_ready, 1)

        @block.gpsimd
        def _(pool):
            pool.iota(g.iota[:, :], [[1, P]], base=0, channel_multiplier=0,
                      allow_small_or_imprecise_dtypes=True)
            pool.wait_ge(built, 1)
            pool.affine_select(out=g.ident[:, :], in_=g.ident[:, :], compare_op=ALU.not_equal, fill=1.0,
                               base=0, pattern=[[-1, P]], channel_multiplier=1)
            pool.affine_select(out=g.before[:, :], in_=g.ones[:, :], compare_op=ALU.is_gt, fill=0.0,
                               base=0, pattern=[[1, P]], channel_multiplier=-1)
            pool.affine_select(out=g.upto[:, :], in_=g.ones[:, :], compare_op=ALU.is_ge, fill=0.0,
                               base=0, pattern=[[1, P]], channel_multiplier=-1)


def bucket(g):
    nc = g.nc
    with Stage(g.nc) as s:
        (loaded, bk_ready, chain, tot_ready, ps_ready, pre_ready, pos_ready, gate) = sems(
            nc, s, "bkt", "loaded bk_ready chain tot_ready ps_ready pre_ready pos_ready gate")
        col_ready, cumc_ready, ge_ready, tid_ps, tid_done = sems(nc, s, "bkt", "col cumc ge tid_ps tid_done")
        copied, = sems(nc, s, "bkt", "copied")
        landed = sems(nc, s, "bkt", "landed0 landed1")
        sb = lambda n, sh, d=F32: s.enter_context(nc.sbuf_tensor(n, sh, d))
        ends = [sb(f"ends{i}", [EP, EC], I32) for i in range(2)]
        bki = sb("bki", [EP, EC], I32)
        bk = [sb(f"bk{i}", [EP, EC]) for i in range(2)]
        oh = [sb(f"oh{i}", [EP, EC]) for i in range(2)]
        cum, term, pos, posi, rowi = (sb("cum", [EP, EC]), sb("term", [EP, EC]), sb("pos", [EP, EC]),
                                      sb("posi", [EP, EC], I32), sb("rowi", [EP, EC], I32))
        tot = sb("tot", [EP, 2, NT])
        nch, nchi = sb("nch", [EP, 2, NT]), sb("nchi", [EP, 2, NT], I32)
        cumc, base = sb("cumc", [EP, 2, NT]), sb("base", [EP, 2, NT])
        coli, colf, cumcol = sb("coli", [NT, 2], I32), sb("colf", [NT, 2]), sb("cumcol", [NT, 2])
        chunk = sb("chunk", [NT, C])
        ge = sb("ge", [NT, 2, C])
        ring = sb("ring", [EP, 2, SC, 3], I32)
        ps = s.enter_context(nc.psum_tensor("ps_bkt", [P, 8, 512], F32))
        block = s.enter_context(nc.Block())
        half = C // 2

        @block.sync
        def _(sp):
            for e, name in zip(ends, ("dst", "src")):
                sp.dma_start(e[:, :], g.inp[name].rearrange("(p c) -> p c", c=EC)).then_inc(loaded, 16)

        n = [0]

        @block.vector
        def _(dve):
            def link(ins):
                n[0] += 1
                ins.then_inc(chain, 1)
                dve.wait_ge(chain, n[0])

            dve.wait_ge(loaded, 32)
            for i in range(2):
                dve.tensor_copy(g.recs[i][:, :, 0], ends[1 - i][:, :])
                dve.tensor_scalar(posi[:, :], ends[i][:, :], P - 1, None, ALU.bitwise_and)
                link(dve.tensor_scalar(bki[:, :], ends[i][:, :], 7, None, ALU.logical_shift_right))
                dve.tensor_copy(g.recs[i][:, :, 1], posi[:, :])
                link(dve.tensor_copy(bk[i][:, :], bki[:, :]))
            n0 = n[0]

            def totals(b, first):
                for i in range(2):
                    dve.wait_ge(chain, n0 + 2 * b + i)
                    dve.tensor_scalar(oh[i][:, :], bk[i][:, :], g.iota[0:EP, bass.ds(b, 1)], 0.0,
                                      ALU.is_equal, ALU.add, accum_out=tot[:, i, bass.ds(b, 1)]).then_inc(chain, 1)
            each(dve, totals, NT)
            n[0] = n0 + 2 * NT
            dve.wait_ge(chain, n[0])
            dve.sem_inc(tot_ready, 1)
            dve.wait_ge(ps_ready, 1)
            all_tot = ps[0:EP, 0, 0:2 * NT].rearrange("p (i b) -> p i b", i=2)
            link(dve.tensor_scalar(nchi[:, :, :], all_tot, float(P - 1), None, ALU.add))
            link(dve.tensor_scalar(nchi[:, :, :], nchi[:, :, :], 7, None, ALU.logical_shift_right))
            link(dve.tensor_copy(nch[:, :, :], nchi[:, :, :]))
            for i in range(2):
                link(dve.tensor_tensor_scan(cumc[:, i, :], nch[:, i, :], nch[:, i, :], 0.0, ALU.add, ALU.max))
            link(dve.tensor_tensor(nch[:, :, :], cumc[:, :, :], nch[:, :, :], ALU.subtract))
            link(dve.scalar_tensor_tensor(base[:, :, :], nch[:, :, :], float(P),
                                          ps[0:EP, 1, 0:2 * NT].rearrange("p (i b) -> p i b", i=2),
                                          ALU.mult, ALU.add))
            link(dve.tensor_scalar(coli[:, :], ps[0:NT, 2, 0:2], float(P - 1), None, ALU.add))
            link(dve.tensor_scalar(coli[:, :], coli[:, :], 7, None, ALU.logical_shift_right))
            dve.tensor_copy(colf[:, :], coli[:, :]).then_inc(col_ready, 1)
            dve.wait_ge(cumc_ready, 1)
            link(dve.tensor_copy(cumcol[:, :], ps[0:NT, 3, 0:2]))
            dve.wait_ge(gate, 1)
            for i in range(2):
                link(dve.tensor_scalar(ge[:, i, :], chunk[:, :], cumcol[:, i:i + 1], None, ALU.is_ge))
            dve.sem_inc(ge_ready, 1)
            for i in range(2):
                for h in range(2):
                    dve.wait_ge(tid_ps, 2 * i + h + 1)
                    link(dve.tensor_scalar(g.tile_of[i][:, h * half:(h + 1) * half],
                                           ps[0:1, 4 + 2 * i + h, 0:half], float(NT - 1), None, ALU.min))
            for i in range(2):
                link(dve.memset(pos[:, :], 0.0))
                m0 = n[0]

                def places(b, first):
                    k = m0 + 4 * b
                    dve.wait_ge(chain, k)
                    dve.tensor_scalar(oh[0][:, :], bk[i][:, :], g.iota[0:EP, bass.ds(b, 1)], None,
                                      ALU.is_equal).then_inc(chain, 1)
                    dve.wait_ge(chain, k + 1)
                    dve.tensor_tensor_scan(cum[:, :], oh[0][:, :], oh[0][:, :], base[:, i, bass.ds(b, 1)],
                                           ALU.add, ALU.max).then_inc(chain, 1)
                    dve.wait_ge(chain, k + 2)
                    dve.tensor_tensor(term[:, :], oh[0][:, :], cum[:, :], ALU.mult).then_inc(chain, 1)
                    dve.wait_ge(chain, k + 3)
                    dve.tensor_tensor(pos[:, :], pos[:, :], term[:, :], ALU.add).then_inc(chain, 1)
                each(dve, places, NT)
                n[0] = m0 + 4 * NT
                dve.wait_ge(chain, n[0])
                link(dve.tensor_scalar(posi[:, :], pos[:, :], 1.0, None, ALU.subtract))
                link(dve.tensor_scalar(rowi[:, :], posi[:, :], 7, None, ALU.logical_shift_right))
                link(dve.tensor_scalar(posi[:, :], posi[:, :], P - 1, None, ALU.bitwise_and))
                dve.scalar_tensor_tensor(g.recs[i][:, :, 2], posi[:, :], float(C), rowi[:, :],
                                         ALU.mult, ALU.add).then_inc(pos_ready, 1)
                dve.wait_ge(pos_ready, i + 1)

        @block.tensor
        def _(pe):
            pe.wait_ge(tot_ready, 1)
            t2 = tot[:, :, :].rearrange("p i b -> p (i b)")
            nc.tensor.matmul(ps[0:EP, 0, 0:2 * NT], g.ones[0:EP, 0:EP], t2, start=True, stop=True)
            nc.tensor.matmul(ps[0:EP, 1, 0:2 * NT], g.before[0:EP, 0:EP], t2, start=True, stop=True)
            for i in range(2):
                last = nc.tensor.matmul(ps[0:NT, 2, i:i + 1], tot[:, i, :], g.ones[0:EP, 0:1], start=True, stop=True)
            last.then_inc(ps_ready, 1)
            pe.wait_ge(col_ready, 1)
            nc.tensor.matmul(ps[0:NT, 3, 0:2], g.upto[0:NT, 0:NT], colf[:, :], start=True, stop=True).then_inc(cumc_ready, 1)
            pe.wait_ge(ge_ready, 1)
            for i in range(2):
                for h in range(2):
                    nc.tensor.matmul(ps[0:1, 4 + 2 * i + h, 0:half], g.ones[0:NT, 0:1],
                                     ge[:, i, h * half:(h + 1) * half], start=True, stop=True).then_inc(tid_ps, 1)

        @block.gpsimd
        def _(pool):
            pool.iota(chunk[:, :], [[1, C]], base=0, channel_multiplier=0,
                      allow_small_or_imprecise_dtypes=True).then_inc(gate, 1)
            pool.wait_ge(pos_ready, 1)
            scatter_pool(g, pool, 0, ring, copied, landed)


def scatter_pool(g, pool, which, ring, copied, landed):
    rows = g.records[which].rearrange("p c w -> (p c) w")
    recs = g.recs[which]

    def body(i, first):
        for h in range(2):
            if not first:
                pool.wait_ge(landed[h], 16 * SC * i)
            pool.tensor_copy(ring[:, h, :, :], recs[:, bass.ds((2 * i + h) * SC, SC), :]).then_inc(copied, 1)
            pool.wait_ge(copied, 2 * i + h + 1)
            pool.sem_inc(g.settled, 1)
            for k in range(SC):
                pool.indirect_dma_start(rows, bass.IndirectOffsetOnAxis(ring[:, h, k, 2:3].bitcast(U32), 0),
                                        ring[:, h, k, 0:2], None).then_inc(landed[h], 16)
    each(pool, body, EC // (2 * SC))
    for h in range(2):
        pool.wait_ge(landed[h], 16 * SC * (EC // (2 * SC)))


class Chain:

    def __init__(self, engine, sem, per):
        self.engine, self.sem, self.per, self.base, self.i, self.m = engine, sem, per, 0, 0, 0

    def step(self, i):
        self.i, self.m = i, 0

    def link(self, instruction):
        self.m += 1
        instruction.then_inc(self.sem, 1)
        self.engine.wait_ge(self.sem, self.base + self.i * self.per + self.m)

    def ended(self):
        assert self.m == self.per, self.m


def tile_at(a, t):
    return a[:, bass.ds(t, 1), :].rearrange("p a b -> p (a b)")


class NodeStage:

    def __init__(self, g, name, s, slices, cols, weights, bias, ln=0, fill=None, turn=None,
                 finish=None, finisher="act", store=None, links=0, setup_dve=None, keep=None, extra=(),
                 stores_turned=False, xt=None, width=P, w=None):
        nc = g.nc
        self.g, self.name = g, name
        names = "loaded chain sd_in sd_out rows_ready turned xt_ready product done ready"
        (loaded, chain, sd_in, sd_out, rows_ready, turned, xt_ready, product, done, ready) = sems(nc, s, name, names)
        stored = [s.semaphore(f"{name}_stored{u}") for u in range(G)] if store else None
        self.done, self.stored = done, stored
        sb = lambda n, sh, d=F32: s.enter_context(nc.sbuf_tensor(f"{name}_{n}", sh, d))
        rows = sb("rows", [P, G, slices * width])
        xt = sb("xt", [width, G, slices, P]) if xt is None else xt
        ps = s.enter_context(nc.psum_tensor(f"{name}_ps", [P, G, 512], F32))
        st, mv, sd = sb("st", [P, G, 6]), sb("mv", [P, G, 2]), sb("sd", [P, G])
        half = sb("half", [P, G, D]) if ln == 2 else None
        w = sb("w", [P, slices, cols]) if w is None else w
        b = sb("b", [1, cols]) if bias is not None else None
        block = s.enter_context(nc.Block())
        nload = len(weights) + (bias is not None) + len(extra)

        @block.sync
        def _(sp):
            for k0, k1, src in weights:
                sp.dma_start(w[:, k0:k1, 0:src.shape[-1]], src.rearrange("(k p) c -> p k c", p=P)).then_inc(loaded, 16)
            if bias is not None:
                sp.dma_start(b[:, :], bias.rearrange("(a c) -> a c", a=1)).then_inc(loaded, 16)
            for dst, src in extra:
                sp.dma_start(dst, src).then_inc(loaded, 16)
            if store:
                def body(i, first):
                    for u in range(G):
                        sp.wait_ge(done, G * i + u + 1)
                        store(sp, u, G * i + u, stored[u])
                each(sp, body, NG)
                for u in range(G):
                    sp.wait_ge(stored[u], 16 * NG * store.dmas)

        @block.vector
        def _(dve):
            if setup_dve:
                setup_dve(dve, w, ready)
            per = 4 * ln + (ln == 2) + (0 if finisher == "act" else links)
            c = Chain(dve, chain, per)

            def norm(i, src, dst, which, inc):
                for u in range(G):
                    ins = dve.bn_stats(st[:, u, :], src(u))
                c.link(ins)
                dve.sem_inc(g.settled, 1)
                for u in range(G):
                    ins = dve.bn_aggr(mv[:, u, :], st[:, u, :])
                c.link(ins)
                c.link(dve.tensor_scalar(mv[:, :, 1], mv[:, :, 1], EPS, None, ALU.add))
                dve.sem_inc(sd_in, 1)
                dve.wait_ge(sd_out, ln * i + which + 1)
                c.link(dve.reciprocal(sd[:, :], sd[:, :]))
                for u in range(G):
                    ins = dve.tensor_scalar(dst(u), src(u), mv[:, u, 0:1], sd[:, u:u + 1], ALU.subtract, ALU.mult)
                    if inc:
                        ins.then_inc(rows_ready, 1)
                return ins

            def body(i, first):
                c.step(i)
                if not first:
                    dve.wait_ge(turned, G * i)
                if ln:
                    src = lambda u: tile_at(g.X, G * i + u)
                    if ln == 2:
                        c.link(norm(i, src, lambda u: half[:, u, :], 0, False))
                        src = lambda u: half[:, u, :]
                    norm(i, src, lambda u: rows[:, u, :], ln - 1, True)
                else:
                    for u in range(G):
                        fill(dve, rows[:, u, :], G * i + u).then_inc(rows_ready, 1)
                if keep:
                    dve.wait_ge(rows_ready, G * (i + 1))
                    keep(dve, rows, i)
                if finisher == "dve":
                    for u in range(G):
                        dve.wait_ge(product, G * i + u + 1)
                        finish(dve, u, G * i + u, i, first, ps[:, u, 0:cols]).then_inc(done, 1)
            each(dve, body, NG)

        def plain(act, dst, src, u, t, i, first):
            return act.copy(dst, src)

        @block.scalar
        def _(act):
            def body(i, first):
                for q in range(ln):
                    act.wait_ge(sd_in, ln * i + q + 1)
                    act.activation(sd[:, :], mv[:, :, 1], ACT.Sqrt).then_inc(sd_out, 1)
                for u in range(G):
                    if stores_turned and not first:
                        act.wait_ge(stored[u], 16 * store.dmas * i)
                    act.wait_ge(turned, G * i + u + 1)
                    src = ps[0:width, u, 0:slices * P].rearrange("p (k c) -> p k c", c=P)
                    (turn or plain)(act, xt[:, u], src, u, G * i + u, i, first).then_inc(xt_ready, 1)
                if finisher == "act":
                    for u in range(G):
                        act.wait_ge(product, G * i + u + 1)
                        if store and not stores_turned and not first:
                            act.wait_ge(stored[u], 16 * store.dmas * i)
                        finish(act, u, G * i + u, i, first, ps[:, u, 0:cols]).then_inc(done, 1)
            if extra:
                act.wait_ge(loaded, 16 * nload)
            each(act, body, NG)

        @block.tensor
        def _(pe):
            pe.wait_ge(loaded, 16 * nload)
            if setup_dve:
                pe.wait_ge(ready, 1)

            def body(i, first):
                for u in range(G):
                    pe.wait_ge(rows_ready, G * i + u + 1)
                    if not first:
                        pe.wait_ge(done, G * (i - 1) + u + 1)
                    for k in range(slices):
                        ins = nc.tensor.transpose(ps[0:width, u, k * P:(k + 1) * P], rows[:, u, k * width:(k + 1) * width], g.ident[:, :])
                    ins.then_inc(turned, 1)
                for u in range(G):
                    pe.wait_ge(xt_ready, G * i + u + 1)
                    for k in range(slices):
                        ins = nc.tensor.matmul(ps[:, u, 0:cols], xt[:, u, k, :], w[:, k, :],
                                               start=k == 0, stop=k == slices - 1 and b is None)
                    if b is not None:
                        ins = nc.tensor.matmul(ps[:, u, 0:cols], g.ones[0:1, :], b[:, :], start=False, stop=True)
                    ins.then_inc(product, 1)
            each(pe, body, NG)


class Store:

    def __init__(self, *pairs):
        self.pairs, self.dmas = pairs, len(pairs)

    def __call__(self, sp, u, t, sem):
        for table, slot in self.pairs:
            sp.dma_start(tile_at(table, t), slot(u)).then_inc(sem, 16)


def tiles_of(table):
    return table.rearrange("(t p) d -> p t d", p=P)


def att_weights(g):
    nc = g.nc
    with Stage(g.nc) as s:
        loaded, zeroed, turned, back, product, kept = sems(nc, s, "att", "loaded zeroed turned back product kept")
        w = s.enter_context(nc.sbuf_tensor("att_w", [P, KD, D], F32))
        wt = s.enter_context(nc.sbuf_tensor("att_wt", [P, KD, D], F32))
        att = s.enter_context(nc.sbuf_tensor("att_v", [P, KD, 2 * HEADS], F32))
        ps = s.enter_context(nc.psum_tensor("att_ps", [P, 3, 512], F32))
        block = s.enter_context(nc.Block())

        @block.sync
        def _(sp):
            sp.dma_start(w[:, :, :], g.inp["L0_gnn_W"].rearrange("(k p) c -> p k c", p=P)).then_inc(loaded, 16)
            sp.wait_ge(zeroed, 1)
            per = P // HD
            for v, name in enumerate(("L0_gnn_att_src", "L0_gnn_att_dst")):
                for h in range(HEADS):
                    p0 = (h % per) * HD
                    sp.dma_start(att[p0:p0 + HD, h // per, v * HEADS + h:v * HEADS + h + 1],
                                 g.inp[name][h, :].rearrange("(c a) -> c a", a=1)).then_inc(loaded, 16)

        @block.vector
        def _(dve):
            dve.memset(att[:, :, :], 0.0).then_inc(zeroed, 1)
            dve.wait_ge(turned, 1)
            for k in range(KD):
                ins = dve.tensor_copy(wt[:, k, :], ps[:, k, 0:D])
            ins.then_inc(back, 1)
            dve.wait_ge(product, 1)
            dve.tensor_copy(g.wa[:, :, :], ps[:, 2, 0:KD * 2 * HEADS].rearrange("p (k c) -> p k c", k=KD))

        @block.tensor
        def _(pe):
            pe.wait_ge(loaded, 16 * (1 + 2 * HEADS))
            for c in range(KD):
                for k in range(KD):
                    ins = nc.tensor.transpose(ps[:, c, k * P:(k + 1) * P], w[:, k, c * P:(c + 1) * P], g.ident[:, :])
            ins.then_inc(turned, 1)
            pe.wait_ge(back, 1)
            for k in range(KD):
                for c in range(KD):
                    ins = nc.tensor.matmul(ps[:, 2, k * 2 * HEADS:(k + 1) * 2 * HEADS], wt[:, c, k * P:(k + 1) * P],
                                           att[:, c, :], start=c == 0, stop=c == KD - 1)
            ins.then_inc(product, 1)


def gat_rows(g, halves):
    with Stage(g.nc) as s:
        out = s.enter_context(g.nc.sbuf_tensor("gr_out", [P, G, D + HEADS], F32))

        def setup_dve(dve, w, ready):
            dve.tensor_copy(w[:, :, D:D + 2 * HEADS], g.wa[:, :, :]).then_inc(ready, 1)

        def finish(act, u, t, i, first, ps):
            act.copy(out[:, u, :], ps[:, 0:D + HEADS])
            return act.copy(tile_at(halves, t), ps[:, D:D + 2 * HEADS])

        NodeStage(g, "gr", s, KD, D + 2 * HEADS, [(0, KD, g.inp["L0_gnn_W"])], None, ln=1, finish=finish,
                  setup_dve=setup_dve,
                  store=Store((tiles_of(g.table), lambda u: out[:, u, 0:D]),
                              (tiles_of(g.score_table), lambda u: out[:, u, D:D + HEADS])))


class EdgeRing:

    def __init__(self, g, name, s, recs, table, ring):
        self.g, self.recs, self.table, self.ring = g, recs, table, ring
        self.idx = s.enter_context(g.nc.sbuf_tensor(f"{name}_idx", [P, R, U], U32))
        self.landed = [s.semaphore(f"{name}_landed{h}") for h in range(R)]
        self.idx_ready, = sems(g.nc, s, name, "idx_ready")

    def indices(self, act, i, h, first):
        if not first:
            act.wait_ge(self.landed[h], 16 * U * i)
        act.copy(self.idx[:, h, :], self.recs[:, bass.ds((R * i + h) * U, U), 0]).then_inc(self.idx_ready, 1)

    def gathers(self, pool, *users):
        width = self.table.shape[-1]

        def body(i, first):
            for h in range(R):
                pool.wait_ge(self.idx_ready, R * i + h + 1)
                if not first:
                    for used, times in users:
                        pool.wait_ge(used, times * (R * i + h - R + 1))
                pool.sem_inc(self.g.settled, 1)
                for k in range(U):
                    pool.indirect_dma_start(self.ring[:, h, k, 0:width], None, self.table,
                                            bass.IndirectOffsetOnAxis(self.idx[:, h, k:k + 1], 0)
                                            ).then_inc(self.landed[h], 16)
        each(pool, body, C // STEP)

    def arrived(self, engine, i, h, late=0):
        engine.wait_ge(self.landed[(h - late) % R], 16 * U * (i + (h - late) // R + 1))


def tile_registers(engine, g, name):
    return [engine.alloc_register(f"{name}{k}") for k in range(U)]


def load_tiles(engine, regs, tile_of, n):
    engine.load(regs, tile_of[0:1, bass.ds(n * U, U)])
    return [engine.snap(r, min_val=0, max_val=NT - 1) for r in regs]


def steps(engine, step, lag):
    last = C // U
    assert lag <= R

    def body(i, first):
        for h in range(R):
            step(R * i + h, i, h, (lambda b, h=h: h >= b) if first else (lambda b: True))
    each(engine, body, C // STEP)
    for h in range(lag):
        step(last + h, C // STEP, h, lambda b, h=h: b > h)


def gat_max(g, halves, scores, table, self_arg):
    nc = g.nc
    with Stage(g.nc) as s:
        (chain, ne_ready, split, turned, pt_ready, masked, reduced, maxed, kept, built, consts, ended) = sems(
            nc, s, "gm", "chain ne_ready split turned pt_ready masked reduced maxed kept built consts ended")
        sb = lambda n, sh, d=F32: s.enter_context(nc.sbuf_tensor("gm_" + n, sh, d))
        ga = sb("ga", [P, R, U, HEADS])
        ne = sb("ne", [P, 2, U, P], BF16)
        parts = sb("parts", [P, 2, U, 3, HEADS], BF16)
        K = U * 3 * HEADS
        pt = sb("pt", [K, 2, P], BF16)
        rest = sb("rest", [P, U, HEADS])
        ident = sb("ident", [P, P], BF16)
        nbig = sb("nbig", [P, HEADS, P], BF16)
        sel = sb("sel", [K, U, HEADS, P], BF16)
        mc = sb("mc", [P, 2, U, HEADS])
        mx = sb("mx", [P, U, NT, HEADS])
        e1 = sb("e1", [P, NT, HEADS])
        ps = s.enter_context(nc.psum_tensor("gm_ps", [P, 4, 512], F32))
        pst = s.enter_context(nc.psum_tensor("gm_pst", [P, 2, 1024], BF16))
        edges = EdgeRing(g, "gm", s, g.rec[0], g.score_table, ga)
        block = s.enter_context(nc.Block())

        @block.gpsimd
        def _(pool):
            pool.memset(sel[:, :, :, :], 0.0).then_inc(built, 1)
            pool.wait_ge(built, 1)
            for part in range(3):
                pool.affine_select(out=sel[:, :, :, :], in_=sel[:, :, :, :], compare_op=ALU.not_equal, fill=1.0,
                                   base=-4 * part, pattern=[[-12, U], [-1, HEADS], [0, P]],
                                   channel_multiplier=1).then_inc(built, 1)
                pool.wait_ge(built, part + 2)
            edges.gathers(pool, (split, 1), (kept, 1))

        @block.scalar
        def _(act):
            def step(n, i, h, known):
                if known(0):
                    edges.indices(act, i, h, not known(R))
                if known(AHEAD):
                    m = n - AHEAD
                    edges.arrived(act, i, h, AHEAD)
                    act.copy(scores[:, bass.ds(m * U, U), :], ga[:, (h - AHEAD) % R, :, :]).then_inc(kept, 1)
                    act.wait_ge(turned, m + 1)
                    act.copy(pt[:, (h - AHEAD) % 2, :], pst[0:K, (h - AHEAD) % 2, 0:P]).then_inc(pt_ready, 1)
            steps(act, step, AHEAD)

        @block.tensor
        def _(pe):
            pe.wait_ge(consts, 1)
            pe.wait_ge(built, 4)

            def body(i, first):
                for h in range(R):
                    n = R * i + h
                    pe.wait_ge(split, n + 1)
                    pe.sem_inc(g.settled, 1)
                    nc.tensor.transpose(pst[0:K, h % 2, 0:P], parts[:, h % 2].rearrange("p k a b -> p (k a b)"),
                                        ident[:, :]).then_inc(turned, 1)
                    for q in range(2):
                        if not (first and h == 0):
                            pe.wait_ge(reduced, 2 * n + q - 1)
                        for k in (2 * q, 2 * q + 1):
                            nc.tensor.matmul(ps[:, k, :], ne[:, h % 2, k, :], nbig[:, :, :].rearrange("p h c -> p (h c)"),
                                             start=True, stop=False)
                        if q == 0:
                            pe.wait_ge(pt_ready, n + 1)
                        for k in (2 * q, 2 * q + 1):
                            for hd in range(HEADS):
                                ins = nc.tensor.matmul(ps[:, k, hd * P:(hd + 1) * P], sel[:, k, hd, :],
                                                       pt[:, h % 2, :], start=False, stop=hd == HEADS - 1)
                        ins.then_inc(masked, 1)
            each(pe, body, C // STEP)

        @block.vector
        def _(dve):
            regs = tile_registers(dve, g, "gm_tile")
            dve.tensor_copy(ident[:, :], g.ident[:, :])
            for hd in range(HEADS):
                ins = dve.tensor_scalar(nbig[:, hd, :], g.ident[:, :], -BIG, None, ALU.mult)
            ins.then_inc(consts, 1)
            for k in range(U):
                ins = dve.tensor_copy(mx[:, k], halves[:, :, 0:HEADS])
            ins.then_inc(ended, 1)
            dve.wait_ge(ended, 1)

            def step(n, i, h, known):
                now, max_now, red_now = known(0), known(2), known(1)
                dst = parts[:, h % 2]
                m = 2 * n

                def into_mx(k):
                    if max_now:
                        a = tile_at(mx[:, k], ts[k])
                        dve.tensor_tensor(a, a, mc[:, h % 2, k, :], ALU.max).then_inc(maxed, 1)

                if now:
                    if known(2):
                        dve.wait_ge(masked, 2 * (n - 1))
                    edges.arrived(dve, i, h)
                    dve.tensor_copy(dst[:, :, 0, :], ga[:, h]).then_inc(chain, 1)
                    dve.tensor_tensor(ne[:, h % 2], g.iota[:, None, :].broadcast_to([P, U, P]),
                                      g.rec[0][:, bass.ds(n * U, U), 1].unsqueeze(2).broadcast_to([P, U, P]),
                                      ALU.not_equal)
                if max_now:
                    ts = load_tiles(dve, regs, g.tile_of[0], n - 2)
                if now:
                    dve.wait_ge(chain, m + 1)
                    if known(1):
                        dve.wait_ge(split, n)
                    dve.tensor_tensor(rest[:, :, :], ga[:, h], dst[:, :, 0, :], ALU.subtract).then_inc(chain, 1)
                if max_now:
                    dve.wait_ge(reduced, 2 * (n - 1))
                    if known(3):
                        dve.wait_ge(maxed, U * (n - 2))
                into_mx(0)
                if now:
                    dve.wait_ge(chain, m + 2)
                    dve.tensor_copy(dst[:, :, 1, :], rest[:, :, :]).then_inc(ne_ready, 1)
                into_mx(1)
                into_mx(2)
                if now:
                    dve.wait_ge(ne_ready, n + 1)
                    dve.tensor_tensor(dst[:, :, 2, :], rest[:, :, :], dst[:, :, 1, :], ALU.subtract).then_inc(split, 1)
                into_mx(3)
                if red_now:
                    for q in range(2):
                        dve.wait_ge(masked, 2 * (n - 1) + q + 1)
                        if q == 0 and known(3):
                            dve.wait_ge(maxed, U * (n - 2))
                        dve.tensor_reduce(mc[:, (h - 1) % 2, 2 * q:2 * q + 2, :].rearrange("p k h -> p (k h)"),
                                          ps[:, 2 * q:2 * q + 2, :].rearrange("p k (h c) -> p (k h) c", c=P),
                                          AX.X, ALU.max).then_inc(reduced, 1)
            steps(dve, step, 2)
            dve.wait_ge(maxed, C)
            c = Chain(dve, chain, 5 + U - 1)
            c.base = 2 * (C // U)
            c.step(0)
            own = halves[:, :, HEADS:2 * HEADS]
            dve.tensor_copy(table[:, :, 0:HEADS], own)
            for k in range(1, U):
                c.link(dve.tensor_tensor(mx[:, 0], mx[:, 0], mx[:, k], ALU.max))
            c.link(dve.tensor_tensor(e1[:, :, :], mx[:, 0], own, ALU.add))
            c.link(dve.scalar_tensor_tensor(table[:, :, HEADS:2 * HEADS], e1[:, :, :], SLOPE, e1[:, :, :],
                                            ALU.mult, ALU.max))
            c.link(dve.tensor_tensor(e1[:, :, :], halves[:, :, 0:HEADS], own, ALU.add))
            c.link(dve.scalar_tensor_tensor(e1[:, :, :], e1[:, :, :], SLOPE, e1[:, :, :], ALU.mult, ALU.max))
            c.link(dve.tensor_tensor(self_arg[:, :, :], e1[:, :, :], table[:, :, HEADS:2 * HEADS], ALU.subtract))
            c.ended()


def gat_sum(g, scores, table, self_arg, acc):
    nc = g.nc
    with Stage(g.nc) as s:
        (chain, oh_ready, turned, oht_ready, ohf_ready, spread, arg_ready, exp_ready, weighted, product, added,
         loaded, self_exp, begun) = sems(nc, s, "gs", "chain oh_ready turned oht_ready ohf_ready spread arg_ready "
                                         "exp_ready weighted product added loaded self_exp begun")
        sb = lambda n, sh, d=F32: s.enter_context(nc.sbuf_tensor("gs_" + n, sh, d))
        rows = sb("rows", [P, R, U, D])
        oh = sb("oh", [P, 2, U, P], BF16)
        ohf, oht = sb("ohf", [P, 2, U, P]), sb("oht", [P, 2, U, P])
        wr = sb("wr", [P, 2, U, D + HEADS])
        arg = sb("arg", [P, U, HEADS])
        ident = sb("ident", [P, P], BF16)
        ps = s.enter_context(nc.psum_tensor("gs_ps", [P, 6, 512], F32))
        pst = s.enter_context(nc.psum_tensor("gs_pst", [P, 2, 1024], BF16))
        edges = EdgeRing(g, "gs", s, g.rec[0], g.table, rows)
        block = s.enter_context(nc.Block())

        @block.sync
        def _(sp):
            sp.dma_start(acc[:, :, 0:D], tiles_of(g.table)).then_inc(loaded, 16)

        @block.gpsimd
        def _(pool):
            edges.gathers(pool, (weighted, U))

        @block.scalar
        def _(act):
            act.activation(acc[:, :, D:D + HEADS], self_arg[:, :, :], ACT.Exp).then_inc(self_exp, 1)

            def step(n, i, h, known):
                if known(0):
                    edges.indices(act, i, h, not known(R))
                if known(AHEAD):
                    m, q = n - AHEAD, (h - AHEAD) % 2
                    act.wait_ge(turned, m + 1)
                    act.copy(oht[:, q].rearrange("p k c -> p (k c)"), pst[:, q, 0:U * P]).then_inc(oht_ready, 1)
                    if known(AHEAD + 2):
                        act.wait_ge(product, (m - 1) * U)
                    act.copy(ohf[:, q], oh[:, q]).then_inc(ohf_ready, 1)
                    act.wait_ge(arg_ready, m + 1)
                    act.activation(wr[:, q, :, D:D + HEADS], arg[:, :, :], ACT.Exp).then_inc(exp_ready, 1)
            steps(act, step, AHEAD)

        @block.tensor
        def _(pe):
            regs = tile_registers(pe, g, "gs_ptile")
            pe.wait_ge(begun, 1)

            def step(n, i, h, known):
                def out(k):
                    if known(1):
                        pe.wait_ge(weighted, (n - 1) * U + k + 1)
                        if known(2):
                            pe.wait_ge(added, (n - 2) * U + k + 1)
                        nc.tensor.matmul(ps[:, 2 + k, 0:D + HEADS], ohf[:, (h - 1) % 2, k, :], wr[:, (h - 1) % 2, k, :],
                                         start=True, stop=True).then_inc(product, 1)

                if known(0):
                    pe.wait_ge(oh_ready, n + 1)
                    for k in range(U):
                        ins = nc.tensor.transpose(pst[:, h % 2, k * P:(k + 1) * P], oh[:, h % 2, k, :], ident[:, :])
                    ins.then_inc(turned, 1)
                    ts = load_tiles(pe, regs, g.tile_of[0], n)
                if known(1):
                    pe.wait_ge(ohf_ready, n)
                out(0)
                if known(0):
                    pe.wait_ge(oht_ready, n + 1)
                    for k in range(U):
                        ins = nc.tensor.matmul(ps[:, h % 2, k * 2 * HEADS:(k + 1) * 2 * HEADS], oht[:, h % 2, k, :],
                                               tile_at(table, ts[k]), start=True, stop=True)
                    ins.then_inc(spread, 1)
                for k in range(1, U):
                    out(k)
            steps(pe, step, 1)

        @block.vector
        def _(dve):
            regs = tile_registers(dve, g, "gs_tile")
            dve.tensor_copy(ident[:, :], g.ident[:, :])
            dve.wait_ge(loaded, 16)
            dve.wait_ge(self_exp, 1)
            dve.tensor_tensor(acc[:, :, 0:D].rearrange("p t (h c) -> p t h c", h=HEADS),
                              acc[:, :, 0:D].rearrange("p t (h c) -> p t h c", h=HEADS),
                              acc[:, :, D:D + HEADS].unsqueeze(3).broadcast_to([P, NT, HEADS, HD]),
                              ALU.mult).then_inc(begun, 1)
            dve.wait_ge(begun, 1)
            links = 3

            def step(n, i, h, known):
                new, weigh, add = known(0), known(1), known(2)
                w = wr[:, (h - 1) % 2]
                own = ps[:, h % 2, 0:U * 2 * HEADS].rearrange("p (k c) -> p k c", k=U)

                def weight(k):
                    if weigh:
                        dve.tensor_tensor(w[:, k, 0:D].rearrange("p (h c) -> p h c", h=HEADS),
                                          rows[:, (h - 1) % R, k, :].rearrange("p (h c) -> p h c", h=HEADS),
                                          w[:, k, D:D + HEADS].unsqueeze(2).broadcast_to([P, HEADS, HD]),
                                          ALU.mult).then_inc(weighted, 1)

                def add_sum(k):
                    if add:
                        dve.wait_ge(product, (n - 2) * U + k + 1)
                        if known(3) or k:
                            dve.wait_ge(added, (n - 2) * U + k)
                        a = tile_at(acc, ts[k])
                        dve.tensor_tensor(a, a, ps[:, 2 + k, 0:D + HEADS], ALU.add).then_inc(added, 1)

                if new:
                    if known(2):
                        dve.wait_ge(turned, n - 1)
                        dve.wait_ge(ohf_ready, n - 1)
                    dve.tensor_tensor(oh[:, h % 2], g.iota[:, None, :].broadcast_to([P, U, P]),
                                      g.rec[0][:, bass.ds(n * U, U), 1].unsqueeze(2).broadcast_to([P, U, P]),
                                      ALU.is_equal).then_inc(oh_ready, 1)
                if add:
                    ts = load_tiles(dve, regs, g.tile_of[0], n - 2)
                if weigh:
                    dve.wait_ge(exp_ready, n)
                    edges.arrived(dve, i, h, 1)
                weight(0)
                add_sum(0)
                weight(1)
                add_sum(1)
                weight(2)
                add_sum(2)
                if new:
                    dve.wait_ge(spread, n + 1)
                    dve.tensor_tensor(arg[:, :, :], scores[:, bass.ds(n * U, U), :], own[:, :, 0:HEADS],
                                      ALU.add).then_inc(chain, 1)
                weight(3)
                if new:
                    dve.wait_ge(chain, links * n + 1)
                    dve.scalar_tensor_tensor(arg[:, :, :], arg[:, :, :], SLOPE, arg[:, :, :], ALU.mult,
                                             ALU.max).then_inc(chain, 1)
                add_sum(3)
                if new:
                    dve.wait_ge(chain, links * n + 2)
                    dve.tensor_tensor(arg[:, :, :], arg[:, :, :], own[:, :, HEADS:2 * HEADS],
                                      ALU.subtract).then_inc(chain, 1)
                    dve.wait_ge(chain, links * n + 3)
                    dve.tensor_scalar(arg[:, :, :], arg[:, :, :], 0.0, None, ALU.min).then_inc(arg_ready, 1)
            steps(dve, step, 2)


def gat_finish(g, acc):
    nc = g.nc
    with Stage(g.nc) as s:
        loaded, chain, summed = sems(nc, s, "gf", "loaded chain summed")
        bias = s.enter_context(nc.sbuf_tensor("gf_bias", [P, D], F32))
        den = s.enter_context(nc.sbuf_tensor("gf_den", [P, NT, HEADS], F32))
        block = s.enter_context(nc.Block())

        @block.sync
        def _(sp):
            sp.dma_start(bias[:, :], g.inp["L0_gnn_bias"].rearrange("(a c) -> a c", a=1).broadcast_to([P, D])).then_inc(loaded, 16)

        @block.vector
        def _(dve):
            dve.tensor_scalar(den[:, :, :], acc[:, :, D:D + HEADS], 1e-16, None, ALU.add).then_inc(chain, 1)
            dve.wait_ge(chain, 1)
            dve.reciprocal(den[:, :, :], den[:, :, :]).then_inc(chain, 1)
            dve.wait_ge(chain, 2)
            dve.wait_ge(loaded, 16)
            c = Chain(dve, chain, 3)
            c.base = 2

            def body(i, first):
                c.step(i)
                a = acc[:, bass.ds(i * G, G), 0:D]
                ah = a.rearrange("p t (h c) -> p t h c", h=HEADS)
                x = g.X[:, bass.ds(i * G, G), :]
                c.link(dve.tensor_tensor(ah, ah, den[:, bass.ds(i * G, G), :].unsqueeze(3).broadcast_to([P, G, HEADS, HD]), ALU.mult))
                c.link(dve.tensor_tensor(a, a, bias[:, None, :].broadcast_to([P, G, D]), ALU.add))
                c.link(dve.scalar_tensor_tensor(x, a, 0.0, x, ALU.max, ALU.add))
            each(dve, body, NG)



def column(v):
    return v.rearrange("(k p) -> p k", p=P)


def moe0_rows(g, logits):
    nc = g.nc
    with Stage(nc) as s:
        gamma = s.enter_context(nc.sbuf_tensor("mr_gamma", [P, KD], F32))
        beta = s.enter_context(nc.sbuf_tensor("mr_beta", [P, KD], F32))

        def turn(act, dst, src, u, t, i, first):
            for k in range(KD):
                ins = act.activation(dst[:, k, :], src[:, k, :], ACT.Identity, bias=beta[:, k:k + 1], scale=gamma[:, k:k + 1])
            return ins

        def finish(act, u, t, i, first, ps):
            return act.copy(tile_at(logits, t), ps)

        columns = g.xt.rearrange("p k (t c) -> p t k c", c=P)

        class StoreTurned:
            dmas = 1

            def __call__(self, sp, u, t, sem):
                sp.dma_start(columns[:, bass.ds(t, 1), :, :].rearrange("p a k c -> p (a k) c"), turned_rows[:, u]).then_inc(sem, 16)

        turned_rows = s.enter_context(nc.sbuf_tensor("mr_xt", [P, G, KD, P], F32))
        NodeStage(g, "mr", s, KD, NE, [(0, KD, g.inp["L0_ffn_Wr"])], g.inp["L0_ffn_br"], ln=2, turn=turn,
                  finish=finish, store=StoreTurned(), stores_turned=True, xt=turned_rows,
                  extra=[(gamma[:, :], column(g.inp["L0_ffn_gamma"])), (beta[:, :], column(g.inp["L0_ffn_beta"]))])


class Small:

    def __init__(self, nc, s, name, dve_sem):
        self.nc, self.s, self.name, self.sem, self.n, self.made = nc, s, name, dve_sem, 0, 0

    def new(self, shape, dtype=F32):
        self.made += 1
        return self.s.enter_context(self.nc.sbuf_tensor(f"{self.name}_{self.made}", shape, dtype))

    def link(self, dve, ins):
        self.n += 1
        ins.then_inc(self.sem, 1)
        dve.wait_ge(self.sem, self.n)


def first_max(dve, v, logits, less8, tmp, best, oh, mx):
    v.link(dve, dve.tensor_reduce(mx[:, :], logits[:, :, :], AX.X, ALU.max))
    v.link(dve, dve.tensor_tensor(tmp[:, :, :], logits[:, :, :], mx[:, :].unsqueeze(2).broadcast_to([P, NT, NE]), ALU.is_equal))
    v.link(dve, dve.tensor_tensor(tmp[:, :, :], tmp[:, :, :], less8[:, None, :].broadcast_to([P, NT, NE]), ALU.mult))
    v.link(dve, dve.tensor_reduce(best[:, :], tmp[:, :, :], AX.X, ALU.min))
    v.link(dve, dve.tensor_tensor(oh[:, :, :], less8[:, None, :].broadcast_to([P, NT, NE]),
                                  best[:, :].unsqueeze(2).broadcast_to([P, NT, NE]), ALU.is_equal))


def moe0_pick(g, logits, share):
    nc = g.nc
    with Stage(nc) as s:
        steps, diff_ready, exp_ready = sems(nc, s, "mp", "steps diff_ready exp_ready")
        v = Small(nc, s, "mp", steps)
        less8, tmp, rest, oh1, oh2 = v.new([P, NE]), v.new([P, NT, NE]), v.new([P, NT, NE]), v.new([P, NT, NE]), v.new([P, NT, NE])
        best, m1, m2, e2, w1 = (v.new([P, NT]) for _ in range(5))
        block = s.enter_context(nc.Block())

        @block.vector
        def _(dve):
            v.link(dve, dve.tensor_scalar(less8[:, :], g.iota[:, 0:NE], float(NE), None, ALU.subtract))
            first_max(dve, v, logits, less8, tmp, best, oh1, m1)
            v.link(dve, dve.scalar_tensor_tensor(rest[:, :, :], oh1[:, :, :], -BIG, logits[:, :, :], ALU.mult, ALU.add))
            first_max(dve, v, rest, less8, tmp, best, oh2, m2)
            dve.tensor_tensor(e2[:, :], m2[:, :], m1[:, :], ALU.subtract).then_inc(diff_ready, 1)
            dve.wait_ge(exp_ready, 1)
            v.link(dve, dve.tensor_scalar(w1[:, :], e2[:, :], 1.0, None, ALU.add))
            v.link(dve, dve.reciprocal(w1[:, :], w1[:, :]))
            v.link(dve, dve.tensor_tensor(e2[:, :], e2[:, :], w1[:, :], ALU.mult))
            v.link(dve, dve.tensor_tensor(oh1[:, :, :], oh1[:, :, :], w1[:, :].unsqueeze(2).broadcast_to([P, NT, NE]), ALU.mult))
            v.link(dve, dve.tensor_tensor(oh2[:, :, :], oh2[:, :, :], e2[:, :].unsqueeze(2).broadcast_to([P, NT, NE]), ALU.mult))
            dve.tensor_tensor(share[:, :, :], oh1[:, :, :], oh2[:, :, :], ALU.add)

        @block.scalar
        def _(act):
            act.wait_ge(diff_ready, 1)
            act.activation(e2[:, :], e2[:, :], ACT.Exp).then_inc(exp_ready, 1)


def moe0_bias(g, share):
    nc = g.nc
    with Stage(nc) as s:
        def fill(dve, dst, t):
            return dve.tensor_copy(dst[:, 0:NE], tile_at(share, t))

        def finish(dve, u, t, i, first, ps):
            return dve.tensor_tensor(tile_at(g.X, t), tile_at(g.X, t), ps, ALU.add)

        w = s.enter_context(nc.sbuf_tensor("mb_w", [NE, 1, D], F32))
        NodeStage(g, "mb", s, 1, D, [], None, fill=fill, finish=finish, finisher="dve", width=NE, w=w,
                  extra=[(w[:, 0, :], g.inp["L0_ffn_b2"])])


def moe0(g, share):
    nc = g.nc
    TG = G * P
    HB = TG // 2
    HC = F0 // P
    M = 2 * HC
    with Stage(nc) as s:
        rows_in, hid_done, gelu_done, out_done, added, copied, small = sems(
            nc, s, "m0", "rows_in hid_done gelu_done out_done added copied small")
        w_in = [s.semaphore(f"m0_w{e}") for e in range(NE)]
        landed = sems(nc, s, "m0", "landed0 landed1")
        sb = lambda n, sh, d=F32: s.enter_context(nc.sbuf_tensor("m0_" + n, sh, d))
        w1, w2 = sb("w1", [P, NE, KD, F0]), sb("w2", [P, NE, HC, D])
        b1 = sb("b1", [P, NE, HC])
        xg = sb("xg", [P, KD, TG])
        hid = sb("hid", [P, 2, HC, TG])
        ring = sb("ring", [EP, 2, SC, 3], I32)
        ps = s.enter_context(nc.psum_tensor("m0_ps", [P, 8, 512], F32))
        block = s.enter_context(nc.Block())

        @block.sync
        def _(sp):
            sp.dma_start(b1[:, :, :], g.inp["L0_ffn_b1"].rearrange("e (k p) -> p e k", p=P)).then_inc(small, 16)
            groups = g.xt.rearrange("p k (i c) -> p i k c", c=TG)

            def load(i, first):
                if not first:
                    sp.wait_ge(hid_done, NE * M * i)
                sp.dma_start(xg[:, :, :], groups[:, bass.ds(i, 1), :, :].rearrange("p a k c -> p (a k) c")).then_inc(rows_in, 16)
            load(0, True)
            for e in range(NE):
                sp.dma_start(w1[:, e], g.inp["L0_ffn_W1"][e].rearrange("(k p) c -> p k c", p=P)).then_inc(w_in[e], 16)
                sp.dma_start(w2[:, e], g.inp["L0_ffn_W2"][e].rearrange("(k p) c -> p k c", p=P)).then_inc(w_in[e], 16)
            with sp.Fori(1, NG) as i:
                load(i, False)

        @block.gpsimd
        def _(pool):
            scatter_pool(g, pool, 1, ring, copied, landed)

        @block.tensor
        def _(pe):
            def hidden(i, first, e):
                if first:
                    pe.wait_ge(w_in[e], 32)
                for m in range(M):
                    q = (NE * i + e) * M + m
                    if not first or e or m >= 4:
                        pe.wait_ge(gelu_done, q - 3)
                    hc, half = m // 2, m % 2
                    for k in range(KD):
                        ins = nc.tensor.matmul(ps[:, m % 4, 0:HB], w1[:, e, k, hc * P:(hc + 1) * P],
                                               xg[:, k, half * HB:(half + 1) * HB], start=k == 0, stop=k == KD - 1)
                    ins.then_inc(hid_done, 1)

            def outputs(i, first, e):
                pe.wait_ge(gelu_done, (NE * i + e + 1) * M)
                for u in range(G):
                    r = (NE * i + e) * G + u
                    if not first or e * G + u >= 4:
                        pe.wait_ge(added, r - 3)
                    bank = 4 + (e * G + u) % 4
                    for k in range(HC):
                        ins = nc.tensor.matmul(ps[:, bank, 0:D], hid[:, e % 2, k, u * P:(u + 1) * P],
                                               w2[:, e, k, :], start=k == 0, stop=k == HC - 1)
                    ins.then_inc(out_done, 1)

            def body(i, first):
                pe.wait_ge(rows_in, 16 * (i + 1))
                hidden(i, first, 0)
                for e in range(NE):
                    if e + 1 < NE:
                        hidden(i, first, e + 1)
                    outputs(i, first, e)
            each(pe, body, NG)

        @block.scalar
        def _(act):
            act.wait_ge(small, 16)

            def body(i, first):
                for e in range(NE):
                    if not first or e >= 2:
                        act.wait_ge(out_done, (NE * i + e - 1) * G)
                    for m in range(M):
                        hc, half = m // 2, m % 2
                        act.wait_ge(hid_done, (NE * i + e) * M + m + 1)
                        act.activation(hid[:, e % 2, hc, half * HB:(half + 1) * HB], ps[:, m % 4, 0:HB], ACT.Gelu,
                                       bias=b1[:, e, hc:hc + 1]).then_inc(gelu_done, 1)
            each(act, body, NG)

        @block.vector
        def _(dve):
            def body(i, first):
                for e in range(NE):
                    for u in range(G):
                        r = (NE * i + e) * G + u
                        if not first or e:
                            dve.wait_ge(added, r - G + 1)
                        dve.wait_ge(out_done, r + 1)
                        x = tile_at(g.X, G * i + u)
                        dve.scalar_tensor_tensor(x, ps[:, 4 + (e * G + u) % 4, 0:D],
                                                 tile_at(share, G * i + u)[:, e:e + 1], x,
                                                 ALU.mult, ALU.add).then_inc(added, 1)
            each(dve, body, NG)


def gnn_rows(g):
    with Stage(g.nc) as s:
        def finish(act, u, t, i, first, ps):
            return act.copy(tile_at(g.H, t), ps)

        NodeStage(g, "gi", s, KD, D, [(0, KD, g.inp["L1_gnn_W_in"])], g.inp["L1_gnn_b_in"], ln=1, finish=finish,
                  store=StoreTile(g))


class StoreTile:
    dmas = 1

    def __init__(self, g):
        self.g = g

    def __call__(self, sp, u, t, sem):
        sp.dma_start(tile_at(tiles_of(self.g.table), t), tile_at(self.g.H, t)).then_inc(sem, 16)


def gnn_sum(g, layer, acc):
    nc = g.nc
    W = D + 1
    with Stage(nc) as s:
        oh_ready, product, added, ready, one = sems(nc, s, f"g{layer}", "oh_ready product added ready one")
        sb = lambda n, sh, d=F32: s.enter_context(nc.sbuf_tensor(f"g{layer}_" + n, sh, d))
        rows = sb("rows", [P, R, U, W])
        oh = sb("oh", [P, R, U, P])
        ps = s.enter_context(nc.psum_tensor(f"g{layer}_ps", [P, 8, 512], F32))
        edges = EdgeRing(g, f"g{layer}e", s, g.rec[1], g.table, rows)
        block = s.enter_context(nc.Block())

        @block.gpsimd
        def _(pool):
            edges.gathers(pool, (product, U))

        @block.scalar
        def _(act):
            def body(i, first):
                for h in range(R):
                    edges.indices(act, i, h, first)
            each(act, body, C // STEP)

        @block.tensor
        def _(pe):
            pe.wait_ge(one, 1)

            def body(i, first):
                for h in range(R):
                    n = R * i + h
                    edges.arrived(pe, i, h)
                    pe.wait_ge(oh_ready, n + 1)
                    for k in range(U):
                        if not (first and h < 2):
                            pe.wait_ge(added, (n - 2) * U + k + 1)
                        nc.tensor.matmul(ps[:, 4 * (h % 2) + k, 0:W], oh[:, h, k, :], rows[:, h, k, :],
                                         start=True, stop=True).then_inc(product, 1)
            each(pe, body, C // STEP)

        @block.vector
        def _(dve):
            regs = tile_registers(dve, g, f"g{layer}_tile")
            dve.memset(rows[:, :, :, D:W], 1.0).then_inc(one, 1)
            dve.memset(acc[:, :, :], 0.0).then_inc(ready, 1)
            dve.wait_ge(ready, 1)

            def body(i, first):
                for h in range(R):
                    n = R * i + h
                    if not first:
                        dve.wait_ge(product, (n - R + 1) * U)
                    dve.tensor_tensor(oh[:, h], g.iota[:, None, :].broadcast_to([P, U, P]),
                                      g.rec[1][:, bass.ds(n * U, U), 1].unsqueeze(2).broadcast_to([P, U, P]),
                                      ALU.is_equal).then_inc(oh_ready, 1)
                    ts = load_tiles(dve, regs, g.tile_of[1], n)
                    for k in range(U):
                        dve.wait_ge(product, n * U + k + 1)
                        if not (first and h == 0 and k == 0):
                            dve.wait_ge(added, n * U + k)
                        a = tile_at(acc, ts[k])
                        dve.tensor_tensor(a, a, ps[:, 4 * (h % 2) + k, 0:W], ALU.add).then_inc(added, 1)
            each(dve, body, C // STEP)


def gnn_update(g, layer, acc):
    nc = g.nc
    with Stage(nc) as s:
        inv = s.enter_context(nc.sbuf_tensor(f"gu{layer}_inv", [P, NT, 1], F32))
        step, = sems(nc, s, f"gu{layer}", "step")

        def setup_dve(dve, w, ready):
            dve.tensor_scalar(inv[:, :, :], acc[:, :, D:D + 1], 1.0, None, ALU.max).then_inc(step, 1)
            dve.wait_ge(step, 1)
            dve.reciprocal(inv[:, :, :], inv[:, :, :]).then_inc(step, 1)
            dve.wait_ge(step, 2)
            dve.sem_inc(ready, 1)

        def fill(dve, dst, t):
            dve.tensor_scalar(dst[:, 0:D], tile_at(acc, t)[:, 0:D], tile_at(inv, t), None, ALU.mult)
            return dve.tensor_copy(dst[:, D:2 * D], tile_at(g.H, t))

        def finish(act, u, t, i, first, ps):
            return act.activation(tile_at(g.H, t), ps, ACT.Relu)

        NodeStage(g, f"gu{layer}", s, 2 * KD, D,
                  [(0, KD, g.inp["L1_gnn_W_agg"][layer]), (KD, 2 * KD, g.inp["L1_gnn_W_self"][layer])],
                  g.inp["L1_gnn_b_hid"][layer], fill=fill, finish=finish, setup_dve=setup_dve, store=StoreTile(g))


def gnn_out(g):
    with Stage(g.nc) as s:
        def fill(dve, dst, t):
            return dve.tensor_copy(dst, tile_at(g.H, t))

        def finish(dve, u, t, i, first, ps):
            return dve.tensor_tensor(tile_at(g.X, t), tile_at(g.X, t), ps, ALU.add)

        NodeStage(g, "go", s, KD, D, [(0, KD, g.inp["L1_gnn_W_out"])], g.inp["L1_gnn_b_out"], fill=fill,
                  finish=finish, finisher="dve")


def moe1_rows(g, xn, logits):
    with Stage(g.nc) as s:
        def keep(dve, rows, i):
            dve.tensor_copy(xn[:, bass.ds(G * i, G), :], rows[:, :, :])

        def finish(act, u, t, i, first, ps):
            return act.copy(tile_at(logits, t), ps)

        NodeStage(g, "nr", s, KD, NE, [(0, KD, g.inp["L1_ffn_gate_w"])], g.inp["L1_ffn_gate_b"], ln=1, keep=keep,
                  finish=finish)


def moe1_pick(g, logits, prob, put, get):
    nc = g.nc
    with Stage(nc) as s:
        steps, arg_ready, exp_ready, oh_ready, counted, dump_ready = sems(
            nc, s, "np", "steps arg_ready exp_ready oh_ready counted dump_ready")
        v = Small(nc, s, "np", steps)
        less8, tmp, oh, ex, tot, carry = v.new([P, NE]), *(v.new([P, NT, NE]) for _ in range(5))
        best, mx, rank, kept, e0, place = (v.new([P, NT]) for _ in range(6))
        past = v.new([P, NT])
        ps = s.enter_context(nc.psum_tensor("np_ps", [P, 2, 512], F32))
        block = s.enter_context(nc.Block())
        L = NT * NE

        @block.gpsimd
        def _(pool):
            pool.iota(past[:, :], [[P, NT]], base=NE * SLOTS, channel_multiplier=1,
                      allow_small_or_imprecise_dtypes=True).then_inc(dump_ready, 1)

        @block.tensor
        def _(pe):
            pe.wait_ge(oh_ready, 1)
            flat = oh[:, :, :].rearrange("p t e -> p (t e)")
            nc.tensor.matmul(ps[:, 0, 0:L], g.upto[:, :], flat, start=True, stop=True)
            nc.tensor.matmul(ps[:, 1, 0:L], g.ones[:, :], flat, start=True, stop=True).then_inc(counted, 1)

        @block.scalar
        def _(act):
            act.wait_ge(arg_ready, 1)
            act.activation(ex[:, :, :], tmp[:, :, :], ACT.Exp).then_inc(exp_ready, 1)

        @block.vector
        def _(dve):
            def go(ins):
                v.link(dve, ins)
            go(dve.tensor_scalar(less8[:, :], g.iota[:, 0:NE], float(NE), None, ALU.subtract))
            first_max(dve, v, logits, less8, tmp, best, oh, mx)
            dve.sem_inc(oh_ready, 1)
            dve.tensor_tensor(tmp[:, :, :], logits[:, :, :], mx[:, :].unsqueeze(2).broadcast_to([P, NT, NE]),
                              ALU.subtract).then_inc(arg_ready, 1)
            dve.wait_ge(exp_ready, 1)
            go(dve.tensor_reduce(prob[:, :], ex[:, :, :], AX.X, ALU.add))
            go(dve.reciprocal(prob[:, :], prob[:, :]))
            dve.wait_ge(counted, 1)
            go(dve.tensor_copy(tot[:, :, :], ps[:, 1, 0:L].rearrange("p (t e) -> p t e", e=NE)))
            for e in range(NE):
                ins = dve.tensor_tensor_scan(carry[:, :, e], tot[:, :, e], tot[:, :, e], 0.0, ALU.add, ALU.max)
            go(ins)
            go(dve.tensor_tensor(carry[:, :, :], carry[:, :, :], tot[:, :, :], ALU.subtract))
            go(dve.tensor_tensor(carry[:, :, :], carry[:, :, :], ps[:, 0, 0:L].rearrange("p (t e) -> p t e", e=NE), ALU.add))
            go(dve.tensor_tensor(carry[:, :, :], carry[:, :, :], oh[:, :, :], ALU.mult))
            go(dve.tensor_reduce(rank[:, :], carry[:, :, :], AX.X, ALU.add))
            go(dve.tensor_scalar(rank[:, :], rank[:, :], 1.0, None, ALU.subtract))
            go(dve.tensor_scalar(kept[:, :], rank[:, :], float(CAP), None, ALU.is_lt))
            go(dve.tensor_tensor(prob[:, :], prob[:, :], kept[:, :], ALU.mult))
            go(dve.tensor_scalar(e0[:, :], best[:, :], float(NE), float(SLOTS), ALU.add, ALU.mult))
            go(dve.scalar_tensor_tensor(place[:, :], rank[:, :], float(CAP - 1), e0[:, :], ALU.min, ALU.add))
            dve.tensor_copy(get[:, :], place[:, :])
            dve.wait_ge(dump_ready, 1)
            go(dve.tensor_tensor(place[:, :], place[:, :], past[:, :], ALU.subtract))
            go(dve.tensor_tensor(place[:, :], place[:, :], kept[:, :], ALU.mult))
            go(dve.tensor_tensor(place[:, :], place[:, :], past[:, :], ALU.add))
            dve.tensor_copy(put[:, :], place[:, :])


def moe1_send(g, xn, put):
    nc = g.nc
    with Stage(nc) as s:
        sent, = sems(nc, s, "ns", "sent")
        block = s.enter_context(nc.Block())

        @block.gpsimd
        def _(pool):
            for t in range(NT):
                n = P if t < NT - 1 else LAST
                pool.indirect_dma_start(g.slots, bass.IndirectOffsetOnAxis(put[0:n, t:t + 1], 0),
                                        xn[0:n, t, :], None).then_inc(sent, 16)
            pool.wait_ge(sent, 16 * NT)


def moe1(g):
    nc = g.nc
    FC = F1 // P
    HALVES = ((0, 512), (512, CAP - 512))
    HP = len(HALVES) * FC
    with Stage(nc) as s:
        loaded = sems(nc, s, "n1", "loaded0 loaded1")
        stored = sems(nc, s, "n1", "stored0 stored1")
        small, turned, xt_ready, hid_done, relu_done, out_done, out_kept, y_zero = sems(
            nc, s, "n1", "small turned xt_ready hid_done relu_done out_done out_kept y_zero")
        sb = lambda n, sh, d=F32: s.enter_context(nc.sbuf_tensor("n1_" + n, sh, d))
        w1, w2 = sb("w1", [P, 2, KD, F1]), sb("w2", [P, 2, FC, D])
        rows = sb("rows", [P, 2, ST, D])
        xt = sb("xt", [P, KD, SLOTS])
        hid = sb("hid", [P, FC, SLOTS])
        y = sb("y", [P, 2, ST, D])
        b1, b2 = sb("b1", [P, NE, FC]), sb("b2", [1, NE, D])
        ps = s.enter_context(nc.psum_tensor("n1_ps", [P, 8, 512], F32))
        slots = g.slots[0:NE * SLOTS, :].rearrange("(e t p) d -> p e t d", p=P, t=ST)
        results = g.results.rearrange("(e t p) d -> p e t d", p=P, t=ST)
        block = s.enter_context(nc.Block())
        rows_of = lambda st: P if st < ST - 1 else CAP - (ST - 1) * P

        def tile_b2(e):
            return b2[:, bass.ds(e, 1), :].rearrange("p a c -> p (a c)")

        def pairs(engine, body):
            def both(i, first):
                for e2 in range(2):
                    body(i, e2, first)
            each(engine, both, NE // 2)

        @block.sync
        def _(sp):
            sp.dma_start(b1[:, :, :], g.inp["L1_ffn_b1"].rearrange("e (k p) -> p e k", p=P)).then_inc(small, 16)
            sp.dma_start(b2[:, :, :], g.inp["L1_ffn_b2"].rearrange("(a e) d -> a e d", a=1)).then_inc(small, 16)
            w1v = g.inp["L1_ffn_w1"].rearrange("e (k p) c -> p e k c", p=P)
            w2v = g.inp["L1_ffn_w2"].rearrange("e (k p) c -> p e k c", p=P)

            def body(i, e2, first):
                e = 2 * i + e2
                if not first:
                    sp.wait_ge(out_done, (e - 1) * ST)
                for dst, src in ((rows[:, e2], slots), (w1[:, e2], w1v), (w2[:, e2], w2v)):
                    sp.dma_start(dst, src[:, bass.ds(e, 1)].rearrange("p a k c -> p (a k) c")).then_inc(loaded[e2], 16)
            pairs(sp, body)

        @block.gpsimd
        def _(pool):
            def body(i, e2, first):
                e = 2 * i + e2
                pool.wait_ge(out_kept, (e + 1) * ST)
                pool.dma_start(results[:, bass.ds(e, 1)].rearrange("p a k c -> p (a k) c"), y[:, e2]).then_inc(stored[e2], 16)
            pairs(pool, body)
            for e2 in range(2):
                pool.wait_ge(stored[e2], 16 * NE // 2)

        @block.tensor
        def _(pe):
            pe.wait_ge(small, 32)

            def body(i, e2, first):
                e = 2 * i + e2
                pe.wait_ge(loaded[e2], 48 * (i + 1))
                for st in range(ST):
                    if not (first and e2 == 0 and st < 4):
                        pe.wait_ge(xt_ready, e * ST + st - 3)
                    if st == 0 and not (first and e2 == 0):
                        pe.wait_ge(relu_done, e * HP)
                    for k in range(KD):
                        ins = nc.tensor.transpose(ps[:, st % 4, k * P:(k + 1) * P], rows[:, e2, st, k * P:(k + 1) * P], g.ident[:, :])
                    ins.then_inc(turned, 1)
                pe.wait_ge(xt_ready, (e + 1) * ST)
                for m in range(HP):
                    q = e * HP + m
                    fc, (c0, cn) = m // 2, HALVES[m % 2]
                    if m >= 4:
                        pe.wait_ge(relu_done, q - 3)
                    for k in range(KD):
                        ins = nc.tensor.matmul(ps[:, m % 4, 0:cn], w1[:, e2, k, fc * P:(fc + 1) * P],
                                               xt[:, k, c0:c0 + cn], start=k == 0, stop=k == KD - 1)
                    ins.then_inc(hid_done, 1)
                pe.wait_ge(relu_done, (e + 1) * HP)
                for st in range(ST):
                    n = rows_of(st)
                    if not (first and e2 == 0 and st < 4):
                        pe.wait_ge(out_kept, e * ST + st - 3)
                    for k in range(FC):
                        nc.tensor.matmul(ps[0:n, 4 + st % 4, 0:D], hid[:, k, st * P:st * P + n], w2[:, e2, k, :],
                                         start=k == 0, stop=False)
                    nc.tensor.matmul(ps[0:n, 4 + st % 4, 0:D], g.ones[0:1, 0:n], tile_b2(e), start=False,
                                     stop=True).then_inc(out_done, 1)
            pairs(pe, body)

        @block.scalar
        def _(act):
            act.wait_ge(small, 32)

            def body(i, e2, first):
                e = 2 * i + e2
                for m in range(HP):
                    fc, (c0, cn) = m // 2, HALVES[m % 2]
                    act.wait_ge(hid_done, e * HP + m + 1)
                    if m == 0 and not (first and e2 == 0):
                        act.wait_ge(out_done, e * ST)
                    act.sem_inc(g.settled, 1)
                    act.activation(hid[:, fc, c0:c0 + cn], ps[:, m % 4, 0:cn], ACT.Relu,
                                   bias=b1[:, bass.ds(e, 1), fc:fc + 1].rearrange("p a c -> p (a c)")).then_inc(relu_done, 1)
            pairs(act, body)

        @block.vector
        def _(dve):
            def body(i, e2, first):
                e = 2 * i + e2
                for st in range(ST):
                    dve.wait_ge(turned, e * ST + st + 1)
                    if st == 0 and not (first and e2 == 0):
                        dve.wait_ge(hid_done, e * HP)
                    dve.tensor_copy(xt[:, :, st * P:(st + 1) * P],
                                    ps[:, st % 4, 0:D].rearrange("p (k c) -> p k c", k=KD)).then_inc(xt_ready, 1)
                if not first:
                    dve.wait_ge(stored[e2], 16 * i)
                for st in range(ST):
                    n = rows_of(st)
                    dve.wait_ge(out_done, e * ST + st + 1)
                    dve.tensor_copy(y[0:n, e2, st, :], ps[0:n, 4 + st % 4, 0:D]).then_inc(out_kept, 1)
            dve.memset(y[:, :, ST - 1, :], 0.0).then_inc(y_zero, 1)
            dve.wait_ge(y_zero, 1)
            pairs(dve, body)


def zero_slots(g):
    nc = g.nc
    with Stage(nc) as s:
        zeroed, ready = sems(nc, s, "zs", "zeroed ready")
        z = s.enter_context(nc.sbuf_tensor("zs_z", [P, ST, D], F32))
        block = s.enter_context(nc.Block())

        @block.vector
        def _(dve):
            dve.memset(z[:, :, :], 0.0).then_inc(ready, 1)

        @block.sync
        def _(sp):
            sp.wait_ge(ready, 1)
            for e in range(NE):
                sp.dma_start(g.slots[e * SLOTS:(e + 1) * SLOTS, :].rearrange("(p t) d -> p t d", p=P), z[:, :, :]).then_inc(zeroed, 16)
            sp.wait_ge(zeroed, 16 * NE)


def moe1_add(g, prob, get):
    nc = g.nc
    FMAX = 3.4028234e38
    INF = 1e4
    with Stage(nc) as s:
        steps, infs, cleaned, added, stored = sems(nc, s, "na", "steps infs cleaned added stored")
        landed = [s.semaphore(f"na_landed{u}") for u in range(G)]
        sb = lambda n, sh, d=F32: s.enter_context(nc.sbuf_tensor("na_" + n, sh, d))
        y = sb("y", [P, G, D])
        up, down, fin = sb("up", [P, G, D]), sb("down", [P, G, D]), sb("fin", [P, G, D], I32)
        block = s.enter_context(nc.Block())

        @block.gpsimd
        def _(pool):
            def gather(t):
                pool.indirect_dma_start(y[:, t % G, :], None, g.results,
                                        bass.IndirectOffsetOnAxis(get[:, t:t + 1], 0)).then_inc(landed[t % G], 16)

            for t in range(G):
                gather(t)
            for t in range(NT):
                u = t % G
                pool.wait_ge(steps, t + 1)
                if t >= G:
                    pool.wait_ge(added, t - G + 1)
                pool.tensor_scalar(up[:, u, :], y[:, u, :], FMAX, INF, ALU.is_gt, ALU.mult)
                pool.tensor_scalar(down[:, u, :], y[:, u, :], -FMAX, -INF, ALU.is_lt, ALU.mult).then_inc(infs, 1)
                if t + G < NT:
                    pool.wait_ge(added, t + 1)
                    gather(t + G)

        @block.vector
        def _(dve):
            for t in range(NT):
                u = t % G
                dve.wait_ge(landed[u], 16 * (t // G + 1))
                dve.tensor_scalar(y[:, u, :], y[:, u, :], prob[:, t:t + 1], None, ALU.mult).then_inc(steps, 1)
                dve.wait_ge(steps, t + 1)
                dve.tensor_scalar(fin[:, u, :], y[:, u, :], 0.0, 0.0, ALU.mult, ALU.is_equal)
                dve.wait_ge(infs, t + 1)
                dve.tensor_tensor(up[:, u, :], up[:, u, :], down[:, u, :], ALU.add).then_inc(cleaned, 1)
                dve.wait_ge(cleaned, 2 * t + 1)
                dve.copy_predicated(up[:, u, :], fin[:, u, :], y[:, u, :]).then_inc(cleaned, 1)
                dve.wait_ge(cleaned, 2 * t + 2)
                dve.tensor_tensor(g.X[:, t, :], g.X[:, t, :], up[:, u, :], ALU.add).then_inc(added, 1)

        @block.sync
        def _(sp):
            for t in range(NT):
                n = P if t < NT - 1 else LAST
                sp.wait_ge(added, t + 1)
                sp.dma_start(g.out[t * P:t * P + n, :], g.X[0:n, t, :]).then_inc(stored, 16)
            sp.wait_ge(stored, 16 * NT)


def kernel_body(nc, inputs, out, stages):
    g = Ctx(nc, inputs, out)
    with ExitStack() as s:
        sb = lambda n, sh, d=F32: s.enter_context(nc.sbuf_tensor(n, sh, d))
        dr = lambda n, sh, d=F32: nc.dram_tensor(n, sh, d, kind="Internal").ap()
        s.enter_context(nc.allow_non_contiguous_dma("a few vectors of a few hundred elements, put on partitions"))
        g.settled = s.enter_context(nc.semaphore("settled"))
        g.X = sb("X", [P, NT, D])
        g.ones, g.ident, g.iota = sb("ones", [P, P]), sb("ident", [P, P]), sb("iota", [P, P])
        g.before, g.upto = sb("before", [P, P]), sb("upto", [P, P])
        g.wa = sb("wa", [P, KD, 2 * HEADS])
        g.tile_of = [sb(f"tile_of{i}", [1, C], I32) for i in range(2)]
        g.records = [dr(f"records{i}", (P, C, 2), I32) for i in range(2)]
        g.table, g.score_table = dr("table", (NP, D)), dr("score_table", (NP, HEADS))
        g.xt = dr("xt", (P, KD, NP))
        g.slots, g.results = dr("slots", (NE * SLOTS + NP, D)), dr("results", (NE * SLOTS, D))
        alloc = lambda stack, n, sh, d=F32: stack.enter_context(nc.sbuf_tensor(n, sh, d))
        with ExitStack() as s2:
            g.recs = [None, alloc(s2, "recs1", [EP, EC, 3], I32)]
            with ExitStack() as s3:
                g.recs[0] = alloc(s3, "recs0", [EP, EC, 3], I32)
                g.rec = [alloc(s3, "rec0", [P, C, 2], I32)]
                setup(g)
                zero_slots(g)
                if 1 in stages:
                  bucket(g)
                  fetch(g, 0)
                halves = alloc(s3, "halves", [P, NT, 2 * HEADS])
                scores = alloc(s3, "scores", [P, C, HEADS])
                self_arg = alloc(s3, "self_arg", [P, NT, HEADS])
                own = alloc(s3, "own", [P, NT, 2 * HEADS])
                if 2 in stages:
                  att_weights(g)
                  gat_rows(g, halves)
                  gat_max(g, halves, scores, own, self_arg)
                  acc = alloc(s3, "gat_acc", [P, NT, D + HEADS])
                  gat_sum(g, scores, own, self_arg, acc)
                  gat_finish(g, acc)
            if 3 in stages:
                logits, share = alloc(s2, "logits0", [P, NT, NE]), alloc(s2, "share", [P, NT, NE])
                moe0_rows(g, logits)
                moe0_pick(g, logits, share)
                moe0_bias(g, share)
                moe0(g, share)
        if 4 in stages:
            with ExitStack() as s2:
                g.rec = [None, alloc(s2, "rec1", [P, C, 2], I32)]
                g.H = alloc(s2, "H", [P, NT, D])
                fetch(g, 1)
                gnn_rows(g)
                for layer in range(3):
                    with ExitStack() as s3:
                        acc = alloc(s3, f"acc{layer}", [P, NT, D + 1])
                        gnn_sum(g, layer, acc)
                        gnn_update(g, layer, acc)
                gnn_out(g)
        if 5 in stages:
            with ExitStack() as s2:
                prob = alloc(s2, "prob", [P, NT])
                put, get = alloc(s2, "put", [P, NT], U32), alloc(s2, "get", [P, NT], U32)
                with ExitStack() as s3:
                    xn, logits = alloc(s3, "xn", [P, NT, D]), alloc(s3, "logits1", [P, NT, NE])
                    moe1_rows(g, xn, logits)
                    moe1_pick(g, logits, prob, put, get)
                    moe1_send(g, xn, put)
                moe1(g)
                moe1_add(g, prob, get)
        else:
            dump(g)


def fetch(g, which):
    nc = g.nc
    with Stage(g.nc) as s:
        loaded, = sems(nc, s, f"fetch{which}", "loaded")
        block = s.enter_context(nc.Block())

        @block.sync
        def _(sp):
            sp.dma_start(g.rec[which][:, :, :], g.records[which]).then_inc(loaded, 16)
            sp.wait_ge(loaded, 16)


def dump(g):
    nc = g.nc
    with Stage(g.nc) as s:
        stored, = sems(nc, s, "dump", "stored")
        block = s.enter_context(nc.Block())

        @block.sync
        def _(sp):
            o = g.out
            sp.dma_start(o[0:(NT - 1) * P, :].rearrange("(t p) d -> p t d", p=P), g.X[:, 0:NT - 1, :]).then_inc(stored, 16)
            sp.dma_start(o[(NT - 1) * P:N, :], g.X[0:LAST, NT - 1, :]).then_inc(stored, 16)
            sp.wait_ge(stored, 32)


NAMES = ["x", "src", "dst", "L0_gnn_W", "L0_gnn_att_src", "L0_gnn_att_dst", "L0_gnn_bias", "L0_ffn_gamma",
         "L0_ffn_beta", "L0_ffn_Wr", "L0_ffn_br", "L0_ffn_W1", "L0_ffn_b1", "L0_ffn_W2", "L0_ffn_b2",
         "L1_gnn_W_in", "L1_gnn_b_in", "L1_gnn_W_agg", "L1_gnn_W_self", "L1_gnn_b_hid", "L1_gnn_W_out",
         "L1_gnn_b_out", "L1_ffn_gate_w", "L1_ffn_gate_b", "L1_ffn_w1", "L1_ffn_b1", "L1_ffn_w2", "L1_ffn_b2"]


def kernel(**inputs):
    import concourse.bacc as bacc
    from concourse.bass_utils import run_bass_kernel_spmd as run

    nc = bacc.Bacc("TRN2", target_bir_lowering=False, num_devices=1)
    arrays, aps = {}, {}
    for name in NAMES:
        a = np.ascontiguousarray(inputs[name])
        arrays[f"in_{name}"] = a
        aps[name] = nc.dram_tensor(f"in_{name}", a.shape, mybir.dt.from_np(a.dtype), kind="ExternalInput").ap()
    out = nc.dram_tensor("out", (N, D), F32, kind="ExternalOutput").ap()
    kernel_body(nc, aps, out, (1, 2, 3, 4, 5))
    r = run(nc, [arrays], core_ids=[0])
    return r.results[0]["out"]
```

```python
import numpy as np
import concourse.bass as bass
from concourse import mybir
from contextlib import ExitStack

F32 = mybir.dt.float32
BF16 = mybir.dt.bfloat16
I32 = mybir.dt.int32
U32 = mybir.dt.uint32
ALU = mybir.AluOpType
ACT = mybir.ActivationFunctionType
AX = mybir.AxisListType

P = 128
N = 6250
D = 256
KD = D // P
NT = -(-N // P)
NP = NT * P
LAST = N - (NT - 1) * P
E = 106250
EP, EC = 125, 850
U, R = 4, 4
AHEAD = 3
STEP = U * R
C = -(-((E + NT * (P - 1)) // P) // STEP) * STEP
HEADS, HD = 4, D // 4
SLOPE = 0.2
EPS = 1e-5
BIG = 2.0 ** 120
G = 7
NG = NT // G
NE = 8
F0 = 512
F1 = 1024
CAP = -(-N * 5 // (4 * NE))
SLOTS = -(-CAP // P) * P
ST = SLOTS // P
BJ = 7
BP = -(-(-(-E // P)) // BJ)
BLOCKS = BP * BJ
assert C >= -(-E // P) + NT
PLACES = 56
SC = 5


def each(engine, body, n):
    body(0, True)
    with engine.Fori(1, n) as i:
        body(i, False)


class Ctx:

    def __init__(self, nc, inputs, out):
        self.nc, self.inp, self.out = nc, inputs, out


class Stage(ExitStack):

    def __init__(self, nc):
        super().__init__()
        self.nc, self.used = nc, []

    def semaphore(self, name):
        self.used.append(self.nc.alloc_semaphore(name))
        return self.used[-1]

    def __exit__(self, *how):
        super().__exit__(*how)
        if how[0] is None:
            self.nc.clear_and_free_semaphores(self.used)
            self.nc.all_engine_barrier()


def sems(nc, stage, prefix, names):
    return [stage.semaphore(f"{prefix}_{n}") for n in names.split()]


def setup(g):
    nc = g.nc
    with Stage(g.nc) as s:
        built, = sems(nc, s, "set", "built")
        block = s.enter_context(nc.Block())

        @block.vector
        def _(dve):
            dve.memset(g.X[:, NT - 1, :], 0.0)
            dve.memset(g.ones[:, :], 1.0)
            dve.memset(g.ident[:, :], 0.0).then_inc(built, 1)

        @block.gpsimd
        def _(pool):
            pool.iota(g.iota[:, :], [[1, P]], base=0, channel_multiplier=0,
                      allow_small_or_imprecise_dtypes=True)
            pool.wait_ge(built, 1)
            pool.affine_select(out=g.ident[:, :], in_=g.ident[:, :], compare_op=ALU.not_equal, fill=1.0,
                               base=0, pattern=[[-1, P]], channel_multiplier=1)
            pool.affine_select(out=g.before[:, :], in_=g.ones[:, :], compare_op=ALU.is_gt, fill=0.0,
                               base=0, pattern=[[1, P]], channel_multiplier=-1)
            pool.affine_select(out=g.upto[:, :], in_=g.ones[:, :], compare_op=ALU.is_ge, fill=0.0,
                               base=0, pattern=[[1, P]], channel_multiplier=-1)


def edge_blocks(g):
    nc = g.nc
    TOP = float(NT)
    CP = -(-C // P)
    with Stage(nc) as s:
        (padded, front, loaded, chain, counted, prefixed, ge_ready, located, row_ready, tile_row, gathered,
         turned, ready, chunk_ready, checked, x_in) = sems(
            nc, s, "eb", "padded front loaded chain counted prefixed ge_ready located row_ready tile_row "
            "gathered turned ready chunk_ready checked x_in")
        sb = lambda n, sh, d=F32: s.enter_context(nc.sbuf_tensor("eb_" + n, sh, d))
        pads = sb("pads", [1, 2, P * (BLOCKS + 1) - E], I32)
        dst = sb("dst", [BP, BJ, P], I32)
        before = sb("before", [BP, 1], I32)
        down = sb("down", [BP, BJ, P])
        bad, nbad = sb("bad", [BP, 2]), sb("nbad", [1, 1])
        prev = sb("prev", [BP, BJ], I32)
        tiles_i = sb("tiles_i", [BP, 3, BJ], I32)
        tiles = sb("tiles", [BP, 3, BJ])
        n, upto, start = sb("n", [BP, BJ]), sb("upto", [BP, BJ]), sb("start", [BP, BJ])
        two = sb("two", [BP, BJ, 2])
        chunk = sb("chunk", [BP, CP * P])
        ge = sb("ge", [BP, BJ, CP * P])
        rowf, tile = sb("rowf", [1, C]), sb("tile", [P, CP])
        chunkp = sb("chunkp", [P, CP])
        row = sb("row", [P, CP], U32)
        got = sb("got", [P, CP, 2, P], I32)
        ends = sb("ends", [P, CP, 2, P])
        ps = s.enter_context(nc.psum_tensor("eb_ps", [P, 8, 512], F32))
        block = s.enter_context(nc.Block())
        half = C // 2

        @block.sync
        def _(sp):
            for w, name in enumerate(("src", "dst")):
                full = E // P
                sp.dma_start(g.blocks[1:1 + full, w, :], g.inp[name][0:full * P].rearrange("(b c) -> b c", c=P)).then_inc(padded, 16)
                sp.dma_start(g.blocks[1 + full:2 + full, w, 0:E - full * P],
                             g.inp[name][full * P:E].rearrange("(a c) -> a c", a=1)).then_inc(padded, 16)
            sp.wait_ge(front, 1)
            for w in range(2):
                full = E // P
                sp.dma_start(g.blocks[0:1, w, :], pads[:, 0, 0:P]).then_inc(padded, 16)
                sp.dma_start(g.blocks[1 + full:2 + full, w, E - full * P:P], pads[:, w, 0:(full + 1) * P - E]).then_inc(padded, 16)
                sp.dma_start(g.blocks[2 + full:, w, :],
                             pads[:, w, 0:(BLOCKS - full - 1) * P].rearrange("a (b c) -> a b c", c=P)).then_inc(padded, 16)
            sp.wait_ge(padded, 160)
            sp.dma_start(dst[:, :, :], g.blocks[1:, 1, :].rearrange("(p j) c -> p j c", j=BJ)).then_inc(loaded, 16)
            sp.dma_start(before[:, :], g.blocks[0:BLOCKS, 1, P - 1:P].rearrange("(p j) c -> p (j c)", j=BJ)[:, 0:1]).then_inc(loaded, 16)

        @block.scalar
        def _(act):
            x = g.inp["x"]
            act.dma_start(g.X[:, 0:NT - 1, :], x[0:(NT - 1) * P, :].rearrange("(t p) d -> p t d", p=P)).then_inc(x_in, 16)
            act.dma_start(g.X[0:LAST, NT - 1, :], x[(NT - 1) * P:N, :]).then_inc(x_in, 16)
            act.wait_ge(x_in, 32)

        @block.vector
        def _(dve):
            k = [0]

            def link(ins):
                k[0] += 1
                ins.then_inc(chain, 1)
                dve.wait_ge(chain, k[0])

            dve.memset(pads[:, 0, :], 0)
            dve.memset(pads[:, 1, :], 2 ** 20).then_inc(front, 1)
            dve.memset(two[:, :, 0], 1.0)
            dve.wait_ge(loaded, 32)
            dve.tensor_copy(tiles_i[:, 0, :], dst[:, :, 0])
            dve.tensor_copy(tiles_i[:, 1, :], dst[:, :, P - 1])
            dve.tensor_copy(tiles_i[:, 2, 1:BJ], dst[:, 0:BJ - 1, P - 1])
            link(dve.tensor_copy(tiles_i[:, 2, 0:1], before[:, :]))
            dve.tensor_tensor(down[:, :, 0:P - 1], dst[:, :, 0:P - 1], dst[:, :, 1:P], ALU.is_gt)
            link(dve.tensor_tensor(down[:, :, P - 1], tiles_i[:, 2, :], tiles_i[:, 0, :], ALU.is_gt))
            link(dve.tensor_reduce(bad[:, 0:1], down[:, :, :].rearrange("p j c -> p (j c)"), AX.X, ALU.add))
            dve.sem_inc(checked, 1)
            link(dve.tensor_scalar(tiles_i[:, :, :], tiles_i[:, :, :], 7, None, ALU.logical_shift_right))
            link(dve.tensor_scalar(tiles[:, :, :], tiles_i[:, :, :], TOP, None, ALU.min))
            link(dve.tensor_scalar(tiles[:, 1, :], tiles[:, 1, :], 1.0, None, ALU.add))
            dve.tensor_tensor(n[:, :], tiles[:, 1, :], tiles[:, 0, :], ALU.subtract)
            link(dve.tensor_scalar(two[:, :, 1], tiles[:, 2, :], 1.0, None, ALU.add))
            link(dve.tensor_tensor(two[:, :, 1], tiles[:, 0, :], two[:, :, 1], ALU.subtract))
            dve.tensor_copy(two[0:1, 0:1, 1], tiles[0:1, 0, 0:1])
            link(dve.tensor_tensor_scan(upto[:, :], n[:, :], n[:, :], 0.0, ALU.add, ALU.bypass))
            dve.sem_inc(counted, 1)
            link(dve.tensor_tensor(start[:, :], upto[:, :], n[:, :], ALU.subtract))
            dve.wait_ge(prefixed, 1)
            link(dve.tensor_scalar(start[:, :], start[:, :], ps[0:BP, 0, 0:1], None, ALU.add))
            dve.tensor_scalar(g.unsorted[:, :], ps[0:1, 0, 1:2], 1.0, None, ALU.min)
            dve.wait_ge(chunk_ready, 1)
            for j in range(BJ):
                ins = dve.tensor_scalar(ge[:, j, :], chunk[:, :], start[:, j:j + 1], None, ALU.is_ge)
            ins.then_inc(ge_ready, 1)
            dve.wait_ge(located, 1)
            where = ps[:, 1, 0:2 * CP].rearrange("p (c w) -> p c w", w=2)
            dve.tensor_copy(row[:, :], where[:, :, 0]).then_inc(row_ready, 1)
            link(dve.tensor_tensor(tile[:, :], where[:, :, 1], chunkp[:, :], ALU.add))
            link(dve.tensor_scalar(tile[:, :], tile[:, :], float(P), None, ALU.mult))
            dve.wait_ge(tile_row, 1)
            for h in range(2):
                ins = dve.tensor_tensor(rowf[:, h * half:(h + 1) * half], ps[0:1, 2 + h, 0:half], chunk[0:1, h * half:(h + 1) * half], ALU.add)
            link(ins)
            link(dve.tensor_scalar(rowf[:, :], rowf[:, :], 0.0, None, ALU.max))
            dve.tensor_scalar(g.tile_of[0][:, :], rowf[:, :], float(NT - 1), None, ALU.min)
            dve.wait_ge(gathered, 16 * CP)
            dve.tensor_copy(ends[:, :, 0, :], got[:, :, 0, :])
            dve.tensor_tensor(ends[:, :, 1, :], got[:, :, 1, :], tile[:, :].unsqueeze(2).broadcast_to([P, CP, P]),
                              ALU.subtract).then_inc(ready, 1)
            for w in range(2):
                dve.wait_ge(turned, w + 1)
                dve.tensor_copy(g.rec[0][:, :, w], ps[:, 4 + 2 * w:6 + 2 * w, :].rearrange("p b c -> p (b c)")[:, 0:C])

        @block.tensor
        def _(pe):
            pe.wait_ge(checked, 1)
            nc.tensor.matmul(ps[0:1, 0, 1:2], bad[:, 0:1], g.ones[0:BP, 0:1], start=True, stop=True)
            pe.wait_ge(counted, 1)
            nc.tensor.matmul(ps[0:BP, 0, 0:1], g.before[0:BP, 0:BP], upto[:, BJ - 1:BJ], start=True, stop=True).then_inc(prefixed, 1)
            pe.wait_ge(ge_ready, 1)
            for c in range(CP):
                for j in range(BJ):
                    ins = nc.tensor.matmul(ps[:, 1, 2 * c:2 * c + 2], ge[:, j, c * P:(c + 1) * P], two[:, j, :],
                                           start=j == 0, stop=j == BJ - 1)
            ins.then_inc(located, 1)
            for h in range(2):
                for j in range(BJ):
                    ins = nc.tensor.matmul(ps[0:1, 2 + h, 0:half], two[:, j, 1:2], ge[:, j, h * half:(h + 1) * half],
                                           start=j == 0, stop=j == BJ - 1)
            ins.then_inc(tile_row, 1)
            pe.wait_ge(ready, 1)
            for w in range(2):
                for c in range(CP):
                    ins = nc.tensor.transpose(ps[:, 4 + 2 * w + c // 4, (c % 4) * P:(c % 4 + 1) * P], ends[:, c, w, :], g.ident[:, :])
                ins.then_inc(turned, 1)

        @block.gpsimd
        def _(pool):
            pool.iota(chunkp[:, :], [[P, CP]], base=0, channel_multiplier=1, allow_small_or_imprecise_dtypes=True)
            pool.iota(chunk[:, :], [[1, CP * P]], base=0, channel_multiplier=0,
                      allow_small_or_imprecise_dtypes=True).then_inc(chunk_ready, 1)
            pool.wait_ge(row_ready, 1)
            for c in range(CP):
                pool.indirect_dma_start(got[:, c].rearrange("p w c -> p (w c)"), None,
                                        g.blocks.rearrange("b w c -> b (w c)"),
                                        bass.IndirectOffsetOnAxis(row[:, c:c + 1], 0)).then_inc(gathered, 16)


def bucket(g, which):
    nc = g.nc
    scatters = which == 0
    with Stage(g.nc) as s:
        (loaded, chain, tot_ready, ps_ready, pos_ready, gate) = sems(
            nc, s, f"bkt{which}", "loaded chain tot_ready ps_ready pos_ready gate")
        col_ready, cumc_ready, ge_ready, tid_ps = sems(nc, s, f"bkt{which}", "col cumc ge tid_ps")
        copied, fetched, filled, fill_ready = sems(nc, s, f"bkt{which}", "copied fetched filled fill_ready")
        landed = sems(nc, s, f"bkt{which}", "landed0 landed1")
        zero_ready, zeroed = sems(nc, s, f"bkt{which}", "zero_ready zeroed")
        sb = lambda n, sh, d=F32: s.enter_context(nc.sbuf_tensor(f"bkt{which}_{n}", sh, d))
        ends = [sb(f"ends{i}", [EP, EC], I32) for i in range(2)]
        fill = sb("fill", [P, C, 2], I32)
        zero = sb("zero", [P, ST, D])
        local = sb("local", [EP, EC], I32)
        oh, cum, pos = sb("oh", [EP, EC], I32), sb("cum", [EP, EC]), sb("pos", [EP, EC])
        tot = sb("tot", [EP, NT])
        nch, nchi = sb("nch", [EP, NT]), sb("nchi", [EP, NT], I32)
        cumc, base0 = sb("cumc", [EP, NT]), sb("base0", [EP, PLACES])
        coli, colf, cumcol = sb("coli", [NT, 1], I32), sb("colf", [NT, 1]), sb("cumcol", [NT, 1])
        chunk = sb("chunk", [NT, C])
        ge = sb("ge", [NT, C])
        recs = sb("recs", [EP, EC, 3], I32) if scatters else g.recs1
        base = base0 if scatters else g.base1
        ring = sb("ring", [EP, 2, SC, 3], I32)
        ps = s.enter_context(nc.psum_tensor(f"ps_bkt{which}", [P, 8, 512], F32))
        block = s.enter_context(nc.Block())
        half = C // 2
        names = ("dst", "src") if which == 0 else ("src", "dst")

        def needed(engine):
            if not scatters:
                return ExitStack()
            return engine.If(engine.value_load(g.unsorted[0:1, 0:1], min_val=0, max_val=1) > 0)

        @block.sync
        def _(sp):
            for e, name in zip(ends, names):
                sp.dma_start(e[:, :], g.inp[name].rearrange("(p c) -> p c", c=EC)).then_inc(loaded, 16)
            sp.wait_ge(loaded, 32)
            if not scatters:
                sp.wait_ge(zero_ready, 1)
                for e in range(NE):
                    sp.dma_start(g.slots[e * SLOTS:(e + 1) * SLOTS, :].rearrange("(p t) d -> p t d", p=P),
                                 zero[:, :, :]).then_inc(zeroed, 16)
                sp.wait_ge(zeroed, 16 * NE)

        @block.vector
        def _(dve):
            if not scatters:
                dve.memset(zero[:, :, :], 0.0).then_inc(zero_ready, 1)
            with needed(dve):
                n = [0]

                def link(ins):
                    n[0] += 1
                    ins.then_inc(chain, 1)
                    dve.wait_ge(chain, n[0])

                dve.memset(fill[:, :, 0], 0)
                dve.memset(fill[:, :, 1], -1).then_inc(fill_ready, 1)
                link(dve.memset(base[:, :], 0.0))
                dve.wait_ge(loaded, 32)
                dve.tensor_copy(recs[:, :, 0], ends[1][:, :])
                dve.tensor_scalar(local[:, :], ends[0][:, :], P - 1, None, ALU.bitwise_and)
                link(dve.tensor_scalar(recs[:, :, 2], ends[0][:, :], 7, None, ALU.logical_shift_right))
                link(dve.tensor_copy(recs[:, :, 1], local[:, :]))
                n0 = n[0]

                def totals(b, first):
                    dve.wait_ge(chain, n0 + b)
                    dve.tensor_scalar(pos[:, :], recs[:, :, 2], g.iota[0:EP, bass.ds(b, 1)], 0.0,
                                      ALU.is_equal, ALU.add, accum_out=tot[:, bass.ds(b, 1)]).then_inc(chain, 1)
                each(dve, totals, NT)
                n[0] = n0 + NT
                dve.wait_ge(chain, n[0])
                dve.sem_inc(tot_ready, 1)
                dve.wait_ge(ps_ready, 1)
                link(dve.tensor_scalar(nchi[:, :], ps[0:EP, 0, 0:NT], float(P - 1), None, ALU.add))
                link(dve.tensor_scalar(nchi[:, :], nchi[:, :], 7, None, ALU.logical_shift_right))
                link(dve.tensor_copy(nch[:, :], nchi[:, :]))
                link(dve.tensor_tensor_scan(cumc[:, :], nch[:, :], nch[:, :], 0.0, ALU.add, ALU.max))
                link(dve.tensor_tensor(nch[:, :], cumc[:, :], nch[:, :], ALU.subtract))
                link(dve.scalar_tensor_tensor(base[:, 0:NT], nch[:, :], float(P), ps[0:EP, 1, 0:NT], ALU.mult, ALU.add))
                link(dve.tensor_scalar(coli[:, :], ps[0:NT, 2, 0:1], float(P - 1), None, ALU.add))
                link(dve.tensor_scalar(coli[:, :], coli[:, :], 7, None, ALU.logical_shift_right))
                dve.tensor_copy(colf[:, :], coli[:, :]).then_inc(col_ready, 1)
                dve.wait_ge(cumc_ready, 1)
                link(dve.tensor_copy(cumcol[:, :], ps[0:NT, 3, 0:1]))
                dve.wait_ge(gate, 1)
                dve.tensor_scalar(ge[:, :], chunk[:, :], cumcol[:, 0:1], None, ALU.is_ge).then_inc(ge_ready, 1)
                for h in range(2):
                    dve.wait_ge(tid_ps, h + 1)
                    dve.tensor_scalar(g.tile_of[which][:, h * half:(h + 1) * half],
                                      ps[0:1, 4 + h, 0:half], float(NT - 1), None, ALU.min)
                if scatters:
                    link(dve.memset(pos[:, :], 0.0))
                    m0 = n[0]

                    def places(b, first):
                        for m in range(3):
                            places_step(g, dve, chain, m0 + 3 * b, m, b, recs, base, oh, cum, pos)
                    each(dve, places, NT)
                    places_end(dve, chain, m0 + 3 * NT, recs, pos, oh, local, pos_ready)

        @block.tensor
        def _(pe):
            with needed(pe):
                pe.wait_ge(tot_ready, 1)
                nc.tensor.matmul(ps[0:EP, 0, 0:NT], g.ones[0:EP, 0:EP], tot[:, :], start=True, stop=True)
                nc.tensor.matmul(ps[0:EP, 1, 0:NT], g.before[0:EP, 0:EP], tot[:, :], start=True, stop=True)
                nc.tensor.matmul(ps[0:NT, 2, 0:1], tot[:, :], g.ones[0:EP, 0:1], start=True, stop=True).then_inc(ps_ready, 1)
                pe.wait_ge(col_ready, 1)
                nc.tensor.matmul(ps[0:NT, 3, 0:1], g.upto[0:NT, 0:NT], colf[:, :], start=True, stop=True).then_inc(cumc_ready, 1)
                pe.wait_ge(ge_ready, 1)
                for h in range(2):
                    nc.tensor.matmul(ps[0:1, 4 + h, 0:half], g.ones[0:NT, 0:1],
                                     ge[:, h * half:(h + 1) * half], start=True, stop=True).then_inc(tid_ps, 1)

        @block.gpsimd
        def _(pool):
            with needed(pool):
                pool.iota(chunk[:, :], [[1, C]], base=0, channel_multiplier=0,
                          allow_small_or_imprecise_dtypes=True).then_inc(gate, 1)
                pool.wait_ge(fill_ready, 1)
                pool.dma_start(g.records[which], fill[:, :, :]).then_inc(filled, 16)
                pool.wait_ge(filled, 16)
                if scatters:
                    pool.wait_ge(pos_ready, 1)
                    scatter_pool(g, pool, which, recs, ring, copied, landed)
                    pool.dma_start(g.rec[0][:, :, :], g.records[which]).then_inc(fetched, 16)
                    pool.wait_ge(fetched, 16)


def places_step(g, dve, chain, k, m, b, recs, base, oh, cum, pos):
    dve.wait_ge(chain, k + m)
    if m == 0:
        dve.tensor_scalar(oh[:, :], recs[:, :, 2], g.iota[0:EP, bass.ds(b, 1)], None, ALU.is_equal).then_inc(chain, 1)
    elif m == 1:
        dve.tensor_tensor_scan(cum[:, :], oh[:, :], oh[:, :], base[:, bass.ds(b, 1)], ALU.add, ALU.max).then_inc(chain, 1)
    else:
        dve.sem_inc(g.settled, 1)
        dve.copy_predicated(pos[:, :], oh[:, :], cum[:, :]).then_inc(chain, 1)


def places_end(dve, chain, k, recs, pos, row, lane, pos_ready):
    dve.wait_ge(chain, k)
    dve.tensor_scalar(lane[:, :], pos[:, :], 1.0, None, ALU.subtract).then_inc(chain, 1)
    dve.wait_ge(chain, k + 1)
    dve.tensor_scalar(row[:, :], lane[:, :], 7, None, ALU.logical_shift_right).then_inc(chain, 1)
    dve.wait_ge(chain, k + 2)
    dve.tensor_scalar(lane[:, :], lane[:, :], P - 1, None, ALU.bitwise_and).then_inc(chain, 1)
    dve.wait_ge(chain, k + 3)
    dve.scalar_tensor_tensor(recs[:, :, 2], lane[:, :], float(C), row[:, :], ALU.mult, ALU.add).then_inc(pos_ready, 1)


def scatter_pool(g, pool, which, recs, ring, copied, landed):
    rows = g.records[which].rearrange("p c w -> (p c) w")

    def body(i, first):
        for h in range(2):
            if not first:
                pool.wait_ge(landed[h], 16 * SC * i)
            pool.tensor_copy(ring[:, h, :, :], recs[:, bass.ds((2 * i + h) * SC, SC), :]).then_inc(copied, 1)
            pool.wait_ge(copied, 2 * i + h + 1)
            pool.sem_inc(g.settled, 1)
            for k in range(SC):
                pool.indirect_dma_start(rows, bass.IndirectOffsetOnAxis(ring[:, h, k, 2:3].bitcast(U32), 0),
                                        ring[:, h, k, 0:2], None).then_inc(landed[h], 16)
    each(pool, body, EC // (2 * SC))
    for h in range(2):
        pool.wait_ge(landed[h], 16 * SC * (EC // (2 * SC)))


class Chain:

    def __init__(self, engine, sem, per):
        self.engine, self.sem, self.per, self.base, self.i, self.m = engine, sem, per, 0, 0, 0

    def step(self, i):
        self.i, self.m = i, 0

    def link(self, instruction):
        self.m += 1
        instruction.then_inc(self.sem, 1)
        self.engine.wait_ge(self.sem, self.base + self.i * self.per + self.m)

    def ended(self):
        assert self.m == self.per, self.m


def tile_at(a, t):
    return a[:, bass.ds(t, 1), :].rearrange("p a b -> p (a b)")


class NodeStage:

    def __init__(self, g, name, s, slices, cols, weights, bias, ln=0, fill=None, turn=None,
                 finish=None, finisher="act", store=None, links=0, setup_dve=None, keep=None, extra=(),
                 stores_turned=False, xt=None, width=P, w=None, last=None):
        nc = g.nc
        self.g, self.name = g, name
        names = "loaded chain sd_in sd_out rows_ready turned xt_ready product done ready"
        (loaded, chain, sd_in, sd_out, rows_ready, turned, xt_ready, product, done, ready) = sems(nc, s, name, names)
        stored = [s.semaphore(f"{name}_stored{u}") for u in range(G)] if store else None
        summed, = sems(nc, s, name, "summed")
        sb = lambda n, sh, d=F32: s.enter_context(nc.sbuf_tensor(f"{name}_{n}", sh, d))
        rows = sb("rows", [P, G, slices * width])
        xt = sb("xt", [width, G, slices, P]) if xt is None else xt
        ps = s.enter_context(nc.psum_tensor(f"{name}_ps", [P, G, 512], F32))
        st, mv, sd = sb("st", [P, G, 6]), sb("mv", [P, G, 2]), sb("sd", [P, G])
        half = sb("half", [P, G, D]) if ln == 2 else None
        w = sb("w", [P, slices, cols]) if w is None else w
        b = sb("b", [1, cols]) if bias is not None else None
        block = s.enter_context(nc.Block())
        nload = len(weights) + (bias is not None) + len(extra)

        @block.sync
        def _(sp):
            for k0, k1, src in weights:
                sp.dma_start(w[:, k0:k1, 0:src.shape[-1]], src.rearrange("(k p) c -> p k c", p=P)).then_inc(loaded, 16)
            if bias is not None:
                sp.dma_start(b[:, :], bias.rearrange("(a c) -> a c", a=1)).then_inc(loaded, 16)
            for dst, src in extra:
                sp.dma_start(dst, src).then_inc(loaded, 16)
            if store:
                def body(i, first):
                    for u in range(G):
                        sp.wait_ge(done, G * i + u + 1)
                        store(sp, u, G * i + u, stored[u])
                each(sp, body, NG)
                for u in range(G):
                    sp.wait_ge(stored[u], 16 * NG * store.dmas)

        @block.vector
        def _(dve):
            if setup_dve:
                setup_dve(dve, w, ready)
            if extra:
                dve.wait_ge(loaded, 16 * nload)
            per = 4 * ln + (ln == 2) + (0 if finisher == "act" else links)
            c = Chain(dve, chain, per)

            def norm(i, src, dst, which, inc):
                for u in range(G):
                    ins = dve.bn_stats(st[:, u, :], src(u))
                c.link(ins)
                dve.sem_inc(g.settled, 1)
                for u in range(G):
                    ins = dve.bn_aggr(mv[:, u, :], st[:, u, :])
                c.link(ins)
                c.link(dve.tensor_scalar(mv[:, :, 1], mv[:, :, 1], EPS, None, ALU.add))
                dve.sem_inc(sd_in, 1)
                dve.wait_ge(sd_out, ln * i + which + 1)
                c.link(dve.reciprocal(sd[:, :], sd[:, :]))
                for u in range(G):
                    ins = dve.tensor_scalar(dst(u), src(u), mv[:, u, 0:1], sd[:, u:u + 1], ALU.subtract, ALU.mult)
                    if inc:
                        ins.then_inc(rows_ready, 1)
                return ins

            def body(i, first):
                c.step(i)
                if not first:
                    dve.wait_ge(turned, G * i)
                if ln:
                    src = lambda u: tile_at(g.X, G * i + u)
                    if ln == 2:
                        c.link(norm(i, src, lambda u: half[:, u, :], 0, False))
                        src = lambda u: half[:, u, :]
                    norm(i, src, lambda u: rows[:, u, :], ln - 1, True)
                else:
                    for u in range(G):
                        fill(dve, rows[:, u, :], G * i + u).then_inc(rows_ready, 1)
                if keep:
                    dve.wait_ge(rows_ready, G * (i + 1))
                    keep(dve, rows, i)
                if finisher != "act" and not first:
                    finish_group(i - 1)

            def finish_group(i):
                for u in range(G):
                    dve.wait_ge(product, G * i + u + 1)
                    finish(dve, u, G * i + u, i, None, ps[:, u, 0:cols]).then_inc(done if last is None else summed, 1)
            each(dve, body, NG)
            if finisher != "act":
                finish_group(NG - 1)

        def plain(act, dst, src, u, t, i, first):
            return act.copy(dst, src)

        @block.scalar
        def _(act):
            def body(i, first):
                for q in range(ln):
                    act.wait_ge(sd_in, ln * i + q + 1)
                    act.activation(sd[:, :], mv[:, :, 1], ACT.Sqrt).then_inc(sd_out, 1)
                for u in range(G):
                    if stores_turned and not first:
                        act.wait_ge(stored[u], 16 * store.dmas * i)
                    act.wait_ge(turned, G * i + u + 1)
                    src = ps[0:width, u, 0:slices * P].rearrange("p (k c) -> p k c", c=P)
                    (turn or plain)(act, xt[:, u], src, u, G * i + u, i, first).then_inc(xt_ready, 1)
                if finisher == "act":
                    for u in range(G):
                        act.wait_ge(product, G * i + u + 1)
                        if store and not stores_turned and not first:
                            act.wait_ge(stored[u], 16 * store.dmas * i)
                        finish(act, u, G * i + u, i, first, ps[:, u, 0:cols]).then_inc(done, 1)
                if last:
                    for u in range(G):
                        act.wait_ge(summed, G * i + u + 1)
                        last(act, G * i + u).then_inc(done, 1)
            if extra:
                act.wait_ge(loaded, 16 * nload)
            each(act, body, NG)

        @block.tensor
        def _(pe):
            pe.wait_ge(loaded, 16 * nload)
            if setup_dve:
                pe.wait_ge(ready, 1)

            def body(i, first):
                for u in range(G):
                    pe.wait_ge(rows_ready, G * i + u + 1)
                    if not first:
                        pe.wait_ge(done, G * (i - 1) + u + 1)
                    for k in range(slices):
                        ins = nc.tensor.transpose(ps[0:width, u, k * P:(k + 1) * P], rows[:, u, k * width:(k + 1) * width], g.ident[:, :])
                    ins.then_inc(turned, 1)
                for u in range(G):
                    pe.wait_ge(xt_ready, G * i + u + 1)
                    for k in range(slices):
                        ins = nc.tensor.matmul(ps[:, u, 0:cols], xt[:, u, k, :], w[:, k, :],
                                               start=k == 0, stop=k == slices - 1 and b is None)
                    if b is not None:
                        ins = nc.tensor.matmul(ps[:, u, 0:cols], g.ones[0:1, :], b[:, :], start=False, stop=True)
                    ins.then_inc(product, 1)
            each(pe, body, NG)


class Store:

    def __init__(self, *pairs):
        self.pairs, self.dmas = pairs, len(pairs)

    def __call__(self, sp, u, t, sem):
        for table, slot in self.pairs:
            sp.dma_start(tile_at(table, t), slot(u)).then_inc(sem, 16)


def tiles_of(table):
    return table.rearrange("(t p) d -> p t d", p=P)


def att_weights(g):
    nc = g.nc
    with Stage(g.nc) as s:
        loaded, zeroed, turned, back, product, kept = sems(nc, s, "att", "loaded zeroed turned back product kept")
        w = s.enter_context(nc.sbuf_tensor("att_w", [P, KD, D], F32))
        wt = s.enter_context(nc.sbuf_tensor("att_wt", [P, KD, D], F32))
        att = s.enter_context(nc.sbuf_tensor("att_v", [P, KD, 2 * HEADS], F32))
        ps = s.enter_context(nc.psum_tensor("att_ps", [P, 3, 512], F32))
        block = s.enter_context(nc.Block())

        @block.sync
        def _(sp):
            sp.dma_start(w[:, :, :], g.inp["L0_gnn_W"].rearrange("(k p) c -> p k c", p=P)).then_inc(loaded, 16)
            sp.wait_ge(zeroed, 1)
            per = P // HD
            for v, name in enumerate(("L0_gnn_att_src", "L0_gnn_att_dst")):
                for h in range(HEADS):
                    p0 = (h % per) * HD
                    sp.dma_start(att[p0:p0 + HD, h // per, v * HEADS + h:v * HEADS + h + 1],
                                 g.inp[name][h, :].rearrange("(c a) -> c a", a=1)).then_inc(loaded, 16)

        @block.vector
        def _(dve):
            dve.memset(att[:, :, :], 0.0).then_inc(zeroed, 1)
            dve.wait_ge(turned, 1)
            for k in range(KD):
                ins = dve.tensor_copy(wt[:, k, :], ps[:, k, 0:D])
            ins.then_inc(back, 1)
            dve.wait_ge(product, 1)
            dve.tensor_copy(g.wa[:, :, :], ps[:, 2, 0:KD * 2 * HEADS].rearrange("p (k c) -> p k c", k=KD))

        @block.tensor
        def _(pe):
            pe.wait_ge(loaded, 16 * (1 + 2 * HEADS))
            for c in range(KD):
                for k in range(KD):
                    ins = nc.tensor.transpose(ps[:, c, k * P:(k + 1) * P], w[:, k, c * P:(c + 1) * P], g.ident[:, :])
            ins.then_inc(turned, 1)
            pe.wait_ge(back, 1)
            for k in range(KD):
                for c in range(KD):
                    ins = nc.tensor.matmul(ps[:, 2, k * 2 * HEADS:(k + 1) * 2 * HEADS], wt[:, c, k * P:(k + 1) * P],
                                           att[:, c, :], start=c == 0, stop=c == KD - 1)
            ins.then_inc(product, 1)


def gat_rows(g, halves):
    with Stage(g.nc) as s:
        out = s.enter_context(g.nc.sbuf_tensor("gr_out", [P, G, D + HEADS], F32))

        def setup_dve(dve, w, ready):
            dve.tensor_copy(w[:, :, D:D + 2 * HEADS], g.wa[:, :, :]).then_inc(ready, 1)

        def finish(act, u, t, i, first, ps):
            act.copy(out[:, u, :], ps[:, 0:D + HEADS])
            return act.copy(tile_at(halves, t), ps[:, D:D + 2 * HEADS])

        NodeStage(g, "gr", s, KD, D + 2 * HEADS, [(0, KD, g.inp["L0_gnn_W"])], None, ln=1, finish=finish,
                  setup_dve=setup_dve,
                  store=Store((tiles_of(g.table), lambda u: out[:, u, 0:D]),
                              (tiles_of(g.score_table), lambda u: out[:, u, D:D + HEADS])))


class EdgeRing:

    def __init__(self, g, name, s, recs, table, ring):
        self.g, self.recs, self.table, self.ring = g, recs, table, ring
        self.idx = s.enter_context(g.nc.sbuf_tensor(f"{name}_idx", [P, R, U], U32))
        self.landed = [s.semaphore(f"{name}_landed{h}") for h in range(R)]
        self.idx_ready, = sems(g.nc, s, name, "idx_ready")

    def indices(self, act, i, h, first):
        if not first:
            act.wait_ge(self.landed[h], 16 * U * i)
        act.copy(self.idx[:, h, :], self.recs[:, bass.ds((R * i + h) * U, U), 0]).then_inc(self.idx_ready, 1)

    def gathers(self, pool, *users):
        width = self.table.shape[-1]

        def body(i, first):
            for h in range(R):
                pool.wait_ge(self.idx_ready, R * i + h + 1)
                if not first:
                    for used, times in users:
                        pool.wait_ge(used, times * (R * i + h - R + 1))
                pool.sem_inc(self.g.settled, 1)
                for k in range(U):
                    pool.indirect_dma_start(self.ring[:, h, k, 0:width], None, self.table,
                                            bass.IndirectOffsetOnAxis(self.idx[:, h, k:k + 1], 0)
                                            ).then_inc(self.landed[h], 16)
        each(pool, body, C // STEP)

    def arrived(self, engine, i, h, late=0):
        engine.wait_ge(self.landed[(h - late) % R], 16 * U * (i + (h - late) // R + 1))


def tile_registers(engine, g, name):
    return [engine.alloc_register(f"{name}{k}") for k in range(U)]


def load_tiles(engine, regs, tile_of, n):
    engine.load(regs, tile_of[0:1, bass.ds(n * U, U)])
    return [engine.snap(r, min_val=0, max_val=NT - 1) for r in regs]


def steps(engine, step, lag):
    last = C // U
    assert lag <= R

    def body(i, first):
        for h in range(R):
            step(R * i + h, i, h, (lambda b, h=h: h >= b) if first else (lambda b: True))
    each(engine, body, C // STEP)
    for h in range(lag):
        step(last + h, C // STEP, h, lambda b, h=h: b > h)


def gat_max(g, halves, scores, table, self_arg):
    nc = g.nc
    with Stage(g.nc) as s:
        (chain, ne_ready, split, turned, pt_ready, masked, reduced, maxed, kept, built, consts, ended) = sems(
            nc, s, "gm", "chain ne_ready split turned pt_ready masked reduced maxed kept built consts ended")
        sb = lambda n, sh, d=F32: s.enter_context(nc.sbuf_tensor("gm_" + n, sh, d))
        ga = sb("ga", [P, R, U, HEADS])
        ne = sb("ne", [P, 2, U, P], BF16)
        parts = sb("parts", [P, 2, U, 3, HEADS], BF16)
        K = U * 3 * HEADS
        pt = sb("pt", [K, 2, P], BF16)
        rest = sb("rest", [P, U, HEADS])
        ident = sb("ident", [P, P], BF16)
        nbig = sb("nbig", [P, HEADS, P], BF16)
        sel = sb("sel", [K, U, HEADS, P], BF16)
        mc = sb("mc", [P, 2, U, HEADS])
        mx = sb("mx", [P, U, NT, HEADS])
        e1 = sb("e1", [P, NT, HEADS])
        ps = s.enter_context(nc.psum_tensor("gm_ps", [P, 4, 512], F32))
        pst = s.enter_context(nc.psum_tensor("gm_pst", [P, 2, 1024], BF16))
        edges = EdgeRing(g, "gm", s, g.rec[0], g.score_table, ga)
        block = s.enter_context(nc.Block())

        @block.gpsimd
        def _(pool):
            pool.memset(sel[:, :, :, :], 0.0).then_inc(built, 1)
            pool.wait_ge(built, 1)
            for part in range(3):
                pool.affine_select(out=sel[:, :, :, :], in_=sel[:, :, :, :], compare_op=ALU.not_equal, fill=1.0,
                                   base=-4 * part, pattern=[[-12, U], [-1, HEADS], [0, P]],
                                   channel_multiplier=1).then_inc(built, 1)
                pool.wait_ge(built, part + 2)
            edges.gathers(pool, (split, 1), (kept, 1))

        @block.scalar
        def _(act):
            def step(n, i, h, known):
                if known(0):
                    edges.indices(act, i, h, not known(R))
                if known(AHEAD):
                    m = n - AHEAD
                    edges.arrived(act, i, h, AHEAD)
                    act.copy(scores[:, bass.ds(m * U, U), :], ga[:, (h - AHEAD) % R, :, :]).then_inc(kept, 1)
                    act.wait_ge(turned, m + 1)
                    act.copy(pt[:, (h - AHEAD) % 2, :], pst[0:K, (h - AHEAD) % 2, 0:P]).then_inc(pt_ready, 1)
            steps(act, step, AHEAD)

        @block.tensor
        def _(pe):
            pe.wait_ge(consts, 1)
            pe.wait_ge(built, 4)

            def body(i, first):
                for h in range(R):
                    n = R * i + h
                    pe.wait_ge(split, n + 1)
                    pe.sem_inc(g.settled, 1)
                    nc.tensor.transpose(pst[0:K, h % 2, 0:P], parts[:, h % 2].rearrange("p k a b -> p (k a b)"),
                                        ident[:, :]).then_inc(turned, 1)
                    for q in range(2):
                        if not (first and h == 0):
                            pe.wait_ge(reduced, 2 * n + q - 1)
                        for k in (2 * q, 2 * q + 1):
                            nc.tensor.matmul(ps[:, k, :], ne[:, h % 2, k, :], nbig[:, :, :].rearrange("p h c -> p (h c)"),
                                             start=True, stop=False)
                        if q == 0:
                            pe.wait_ge(pt_ready, n + 1)
                        for k in (2 * q, 2 * q + 1):
                            for hd in range(HEADS):
                                ins = nc.tensor.matmul(ps[:, k, hd * P:(hd + 1) * P], sel[:, k, hd, :],
                                                       pt[:, h % 2, :], start=False, stop=hd == HEADS - 1)
                        ins.then_inc(masked, 1)
            each(pe, body, C // STEP)

        @block.vector
        def _(dve):
            regs = tile_registers(dve, g, "gm_tile")
            dve.tensor_copy(ident[:, :], g.ident[:, :])
            for hd in range(HEADS):
                ins = dve.tensor_scalar(nbig[:, hd, :], g.ident[:, :], -BIG, None, ALU.mult)
            ins.then_inc(consts, 1)
            for k in range(U):
                ins = dve.tensor_copy(mx[:, k], halves[:, :, 0:HEADS])
            ins.then_inc(ended, 1)
            dve.wait_ge(ended, 1)

            def step(n, i, h, known):
                now, max_now, red_now = known(0), known(2), known(1)
                dst = parts[:, h % 2]
                m = 2 * n

                def into_mx(k):
                    if max_now:
                        a = tile_at(mx[:, k], ts[k])
                        dve.tensor_tensor(a, a, mc[:, h % 2, k, :], ALU.max).then_inc(maxed, 1)

                if now:
                    if known(2):
                        dve.wait_ge(masked, 2 * (n - 1))
                    edges.arrived(dve, i, h)
                    dve.tensor_copy(dst[:, :, 0, :], ga[:, h]).then_inc(chain, 1)
                    dve.tensor_tensor(ne[:, h % 2], g.iota[:, None, :].broadcast_to([P, U, P]),
                                      g.rec[0][:, bass.ds(n * U, U), 1].unsqueeze(2).broadcast_to([P, U, P]),
                                      ALU.not_equal)
                if max_now:
                    ts = load_tiles(dve, regs, g.tile_of[0], n - 2)
                if now:
                    dve.wait_ge(chain, m + 1)
                    if known(1):
                        dve.wait_ge(split, n)
                    dve.tensor_tensor(rest[:, :, :], ga[:, h], dst[:, :, 0, :], ALU.subtract).then_inc(chain, 1)
                if max_now:
                    dve.wait_ge(reduced, 2 * (n - 1))
                    if known(3):
                        dve.wait_ge(maxed, U * (n - 2))
                into_mx(0)
                if now:
                    dve.wait_ge(chain, m + 2)
                    dve.tensor_copy(dst[:, :, 1, :], rest[:, :, :]).then_inc(ne_ready, 1)
                into_mx(1)
                into_mx(2)
                if now:
                    dve.wait_ge(ne_ready, n + 1)
                    dve.tensor_tensor(dst[:, :, 2, :], rest[:, :, :], dst[:, :, 1, :], ALU.subtract).then_inc(split, 1)
                into_mx(3)
                if red_now:
                    for q in range(2):
                        dve.wait_ge(masked, 2 * (n - 1) + q + 1)
                        if q == 0 and known(3):
                            dve.wait_ge(maxed, U * (n - 2))
                        dve.tensor_reduce(mc[:, (h - 1) % 2, 2 * q:2 * q + 2, :].rearrange("p k h -> p (k h)"),
                                          ps[:, 2 * q:2 * q + 2, :].rearrange("p k (h c) -> p (k h) c", c=P),
                                          AX.X, ALU.max).then_inc(reduced, 1)
            steps(dve, step, 2)
            dve.wait_ge(maxed, C)
            c = Chain(dve, chain, 5 + U - 1)
            c.base = 2 * (C // U)
            c.step(0)
            own = halves[:, :, HEADS:2 * HEADS]
            dve.tensor_copy(table[:, :, 0:HEADS], own)
            for k in range(1, U):
                c.link(dve.tensor_tensor(mx[:, 0], mx[:, 0], mx[:, k], ALU.max))
            c.link(dve.tensor_tensor(e1[:, :, :], mx[:, 0], own, ALU.add))
            c.link(dve.scalar_tensor_tensor(table[:, :, HEADS:2 * HEADS], e1[:, :, :], SLOPE, e1[:, :, :],
                                            ALU.mult, ALU.max))
            c.link(dve.tensor_tensor(e1[:, :, :], halves[:, :, 0:HEADS], own, ALU.add))
            c.link(dve.scalar_tensor_tensor(e1[:, :, :], e1[:, :, :], SLOPE, e1[:, :, :], ALU.mult, ALU.max))
            c.link(dve.tensor_tensor(self_arg[:, :, :], e1[:, :, :], table[:, :, HEADS:2 * HEADS], ALU.subtract))
            c.ended()


def gat_sum(g, scores, table, self_arg, acc):
    nc = g.nc
    with Stage(g.nc) as s:
        (chain, oh_ready, turned, oht_ready, ohf_ready, spread, arg_ready, exp_ready, weighted, product, added,
         loaded, self_exp, begun) = sems(nc, s, "gs", "chain oh_ready turned oht_ready ohf_ready spread arg_ready "
                                         "exp_ready weighted product added loaded self_exp begun")
        sb = lambda n, sh, d=F32: s.enter_context(nc.sbuf_tensor("gs_" + n, sh, d))
        rows = sb("rows", [P, R, U, D])
        oh = sb("oh", [P, 2, U, P], BF16)
        ohf, oht = sb("ohf", [P, 2, U, P]), sb("oht", [P, 2, U, P])
        wr = sb("wr", [P, 2, U, D + HEADS])
        arg = sb("arg", [P, 2, U, HEADS])
        ident = sb("ident", [P, P], BF16)
        ps = s.enter_context(nc.psum_tensor("gs_ps", [P, 6, 512], F32))
        pst = s.enter_context(nc.psum_tensor("gs_pst", [P, 2, 1024], BF16))
        edges = EdgeRing(g, "gs", s, g.rec[0], g.table, rows)
        block = s.enter_context(nc.Block())

        @block.sync
        def _(sp):
            sp.dma_start(acc[:, :, 0:D], tiles_of(g.table)).then_inc(loaded, 16)

        @block.gpsimd
        def _(pool):
            edges.gathers(pool, (weighted, U))

        @block.scalar
        def _(act):
            act.activation(acc[:, :, D:D + HEADS], self_arg[:, :, :], ACT.Exp).then_inc(self_exp, 1)

            def step(n, i, h, known):
                if known(0):
                    edges.indices(act, i, h, not known(R))
                m, q = n - AHEAD, (h - AHEAD) % 2
                if known(AHEAD):
                    act.wait_ge(turned, m + 1)
                    act.copy(oht[:, q].rearrange("p k c -> p (k c)"), pst[:, q, 0:U * P]).then_inc(oht_ready, 1)
                if known(AHEAD + 1):
                    act.wait_ge(arg_ready, m)
                    act.activation(wr[:, 1 - q, :, D:D + HEADS], arg[:, 1 - q], ACT.Exp).then_inc(exp_ready, 1)
                if known(AHEAD):
                    if known(AHEAD + 2):
                        act.wait_ge(product, (m - 1) * U)
                    act.copy(ohf[:, q], oh[:, q]).then_inc(ohf_ready, 1)
            steps(act, step, AHEAD + 1)

        @block.tensor
        def _(pe):
            regs = tile_registers(pe, g, "gs_ptile")
            pe.wait_ge(begun, 1)

            def step(n, i, h, known):
                def out(k):
                    if known(2):
                        pe.wait_ge(weighted, (n - 2) * U + k + 1)
                        if known(3):
                            pe.wait_ge(added, (n - 3) * U + k + 1)
                        nc.tensor.matmul(ps[:, 2 + k, 0:D + HEADS], ohf[:, h % 2, k, :], wr[:, h % 2, k, :],
                                         start=True, stop=True).then_inc(product, 1)

                if known(0):
                    pe.wait_ge(oh_ready, n + 1)
                    for k in range(U):
                        ins = nc.tensor.transpose(pst[:, h % 2, k * P:(k + 1) * P], oh[:, h % 2, k, :], ident[:, :])
                    ins.then_inc(turned, 1)
                    ts = load_tiles(pe, regs, g.tile_of[0], n)
                if known(2):
                    pe.wait_ge(ohf_ready, n - 1)
                out(0)
                out(1)
                if known(0):
                    pe.wait_ge(oht_ready, n + 1)
                    for k in range(U):
                        ins = nc.tensor.matmul(ps[:, h % 2, k * 2 * HEADS:(k + 1) * 2 * HEADS], oht[:, h % 2, k, :],
                                               tile_at(table, ts[k]), start=True, stop=True)
                    ins.then_inc(spread, 1)
                out(2)
                out(3)
            steps(pe, step, 2)

        @block.vector
        def _(dve):
            regs = tile_registers(dve, g, "gs_tile")
            dve.tensor_copy(ident[:, :], g.ident[:, :])
            dve.wait_ge(loaded, 16)
            dve.wait_ge(self_exp, 1)
            dve.tensor_tensor(acc[:, :, 0:D].rearrange("p t (h c) -> p t h c", h=HEADS),
                              acc[:, :, 0:D].rearrange("p t (h c) -> p t h c", h=HEADS),
                              acc[:, :, D:D + HEADS].unsqueeze(3).broadcast_to([P, NT, HEADS, HD]),
                              ALU.mult).then_inc(begun, 1)
            dve.wait_ge(begun, 1)
            links = 3

            def step(n, i, h, known):
                argue, weigh, add = known(1), known(2), known(3)
                q = (h - 1) % 2
                w = wr[:, h % 2]
                own = ps[:, q, 0:U * 2 * HEADS].rearrange("p (k c) -> p k c", k=U)

                def weight(k):
                    if weigh:
                        dve.tensor_tensor(w[:, k, 0:D].rearrange("p (h c) -> p h c", h=HEADS),
                                          rows[:, (h - 2) % R, k, :].rearrange("p (h c) -> p h c", h=HEADS),
                                          w[:, k, D:D + HEADS].unsqueeze(2).broadcast_to([P, HEADS, HD]),
                                          ALU.mult).then_inc(weighted, 1)

                def add_sum(k):
                    if add:
                        dve.wait_ge(product, (n - 3) * U + k + 1)
                        if known(4) or k:
                            dve.wait_ge(added, (n - 3) * U + k)
                        a = tile_at(acc, ts[k])
                        dve.tensor_tensor(a, a, ps[:, 2 + k, 0:D + HEADS], ALU.add).then_inc(added, 1)

                if known(0):
                    if known(2):
                        dve.wait_ge(turned, n - 1)
                        dve.wait_ge(ohf_ready, n - 1)
                    dve.tensor_tensor(oh[:, h % 2], g.iota[:, None, :].broadcast_to([P, U, P]),
                                      g.rec[0][:, bass.ds(n * U, U), 1].unsqueeze(2).broadcast_to([P, U, P]),
                                      ALU.is_equal).then_inc(oh_ready, 1)
                if add:
                    ts = load_tiles(dve, regs, g.tile_of[0], n - 3)
                add_sum(0)
                if argue:
                    dve.wait_ge(spread, n)
                    if known(3):
                        dve.wait_ge(exp_ready, n - 2)
                    dve.tensor_tensor(arg[:, q], scores[:, bass.ds((n - 1) * U, U), :], own[:, :, 0:HEADS],
                                      ALU.add).then_inc(chain, 1)
                if weigh:
                    dve.wait_ge(exp_ready, n - 1)
                    edges.arrived(dve, i, h, 2)
                weight(0)
                if argue:
                    dve.wait_ge(chain, links * (n - 1) + 1)
                    dve.scalar_tensor_tensor(arg[:, q], arg[:, q], SLOPE, arg[:, q], ALU.mult,
                                             ALU.max).then_inc(chain, 1)
                add_sum(1)
                if argue:
                    dve.wait_ge(chain, links * (n - 1) + 2)
                    dve.tensor_tensor(arg[:, q], arg[:, q], own[:, :, HEADS:2 * HEADS],
                                      ALU.subtract).then_inc(chain, 1)
                weight(1)
                if argue:
                    dve.wait_ge(chain, links * (n - 1) + 3)
                    dve.tensor_scalar(arg[:, q], arg[:, q], 0.0, None, ALU.min).then_inc(arg_ready, 1)
                add_sum(2)
                weight(2)
                add_sum(3)
                weight(3)
            steps(dve, step, 3)


def gat_finish(g, acc):
    nc = g.nc
    with Stage(g.nc) as s:
        loaded, chain, summed = sems(nc, s, "gf", "loaded chain summed")
        bias = s.enter_context(nc.sbuf_tensor("gf_bias", [P, D], F32))
        den = s.enter_context(nc.sbuf_tensor("gf_den", [P, NT, HEADS], F32))
        block = s.enter_context(nc.Block())

        @block.sync
        def _(sp):
            sp.dma_start(bias[:, :], g.inp["L0_gnn_bias"].rearrange("(a c) -> a c", a=1).broadcast_to([P, D])).then_inc(loaded, 16)

        @block.vector
        def _(dve):
            dve.tensor_scalar(den[:, :, :], acc[:, :, D:D + HEADS], 1e-16, None, ALU.add).then_inc(chain, 1)
            dve.wait_ge(chain, 1)
            dve.reciprocal(den[:, :, :], den[:, :, :]).then_inc(chain, 1)
            dve.wait_ge(chain, 2)
            dve.wait_ge(loaded, 16)
            c = Chain(dve, chain, 3)
            c.base = 2

            def body(i, first):
                c.step(i)
                a = acc[:, bass.ds(i * G, G), 0:D]
                ah = a.rearrange("p t (h c) -> p t h c", h=HEADS)
                x = g.X[:, bass.ds(i * G, G), :]
                c.link(dve.tensor_tensor(ah, ah, den[:, bass.ds(i * G, G), :].unsqueeze(3).broadcast_to([P, G, HEADS, HD]), ALU.mult))
                c.link(dve.tensor_tensor(a, a, bias[:, None, :].broadcast_to([P, G, D]), ALU.add))
                c.link(dve.scalar_tensor_tensor(x, a, 0.0, x, ALU.max, ALU.add))
            each(dve, body, NG)



def column(v):
    return v.rearrange("(k p) -> p k", p=P)


def moe0_rows(g, logits):
    nc = g.nc
    with Stage(nc) as s:
        gamma = s.enter_context(nc.sbuf_tensor("mr_gamma", [P, KD], F32))
        beta = s.enter_context(nc.sbuf_tensor("mr_beta", [P, KD], F32))

        def turn(act, dst, src, u, t, i, first):
            for k in range(KD):
                ins = act.activation(dst[:, k, :], src[:, k, :], ACT.Identity, bias=beta[:, k:k + 1], scale=gamma[:, k:k + 1])
            return ins

        def finish(dve, u, t, i, first, ps):
            return dve.tensor_copy(tile_at(logits, t), ps)

        columns = g.xt.rearrange("p k (t c) -> p t k c", c=P)

        class StoreTurned:
            dmas = 1

            def __call__(self, sp, u, t, sem):
                sp.dma_start(columns[:, bass.ds(t, 1), :, :].rearrange("p a k c -> p (a k) c"), turned_rows[:, u]).then_inc(sem, 16)

        turned_rows = s.enter_context(nc.sbuf_tensor("mr_xt", [P, G, KD, P], F32))
        NodeStage(g, "mr", s, KD, NE, [(0, KD, g.inp["L0_ffn_Wr"])], None, ln=2, turn=turn,
                  finish=finish, finisher="dve", store=StoreTurned(), stores_turned=True, xt=turned_rows,
                  extra=[(gamma[:, :], column(g.inp["L0_ffn_gamma"])), (beta[:, :], column(g.inp["L0_ffn_beta"]))])


class Small:

    def __init__(self, nc, s, name, dve_sem):
        self.nc, self.s, self.name, self.sem, self.n, self.made = nc, s, name, dve_sem, 0, 0

    def new(self, shape, dtype=F32):
        self.made += 1
        return self.s.enter_context(self.nc.sbuf_tensor(f"{self.name}_{self.made}", shape, dtype))

    def link(self, dve, ins):
        self.n += 1
        ins.then_inc(self.sem, 1)
        dve.wait_ge(self.sem, self.n)


def first_max(dve, v, logits, less8, tmp, best, oh, mx):
    v.link(dve, dve.tensor_reduce(mx[:, :], logits[:, :, :], AX.X, ALU.max))
    v.link(dve, dve.tensor_tensor(tmp[:, :, :], logits[:, :, :], mx[:, :].unsqueeze(2).broadcast_to([P, NT, NE]), ALU.is_equal))
    v.link(dve, dve.tensor_tensor(tmp[:, :, :], tmp[:, :, :], less8[:, None, :].broadcast_to([P, NT, NE]), ALU.mult))
    v.link(dve, dve.tensor_reduce(best[:, :], tmp[:, :, :], AX.X, ALU.min))
    v.link(dve, dve.tensor_tensor(oh[:, :, :], less8[:, None, :].broadcast_to([P, NT, NE]),
                                  best[:, :].unsqueeze(2).broadcast_to([P, NT, NE]), ALU.is_equal))


def moe0_pick(g, logits, share):
    nc = g.nc
    with Stage(nc) as s:
        steps, diff_ready, exp_ready, loaded = sems(nc, s, "mp", "steps diff_ready exp_ready loaded")
        v = Small(nc, s, "mp", steps)
        less8, tmp, rest, oh1, oh2 = v.new([P, NE]), v.new([P, NT, NE]), v.new([P, NT, NE]), v.new([P, NT, NE]), v.new([P, NT, NE])
        best, m1, m2, e2, w1 = (v.new([P, NT]) for _ in range(5))
        bias = v.new([P, 1, NE])
        block = s.enter_context(nc.Block())

        @block.sync
        def _(sp):
            sp.dma_start(bias[:, 0, :], every_partition(g.inp["L0_ffn_br"])).then_inc(loaded, 16)

        @block.vector
        def _(dve):
            dve.wait_ge(loaded, 16)
            v.link(dve, dve.tensor_tensor(logits[:, :, :], logits[:, :, :], bias[:, :, :].broadcast_to([P, NT, NE]), ALU.add))
            v.link(dve, dve.tensor_scalar(less8[:, :], g.iota[:, 0:NE], float(NE), None, ALU.subtract))
            first_max(dve, v, logits, less8, tmp, best, oh1, m1)
            v.link(dve, dve.scalar_tensor_tensor(rest[:, :, :], oh1[:, :, :], -BIG, logits[:, :, :], ALU.mult, ALU.add))
            first_max(dve, v, rest, less8, tmp, best, oh2, m2)
            dve.tensor_tensor(e2[:, :], m2[:, :], m1[:, :], ALU.subtract).then_inc(diff_ready, 1)
            dve.wait_ge(exp_ready, 1)
            v.link(dve, dve.tensor_scalar(w1[:, :], e2[:, :], 1.0, None, ALU.add))
            v.link(dve, dve.reciprocal(w1[:, :], w1[:, :]))
            v.link(dve, dve.tensor_tensor(e2[:, :], e2[:, :], w1[:, :], ALU.mult))
            v.link(dve, dve.tensor_tensor(oh1[:, :, :], oh1[:, :, :], w1[:, :].unsqueeze(2).broadcast_to([P, NT, NE]), ALU.mult))
            v.link(dve, dve.tensor_tensor(oh2[:, :, :], oh2[:, :, :], e2[:, :].unsqueeze(2).broadcast_to([P, NT, NE]), ALU.mult))
            dve.tensor_tensor(share[:, :, :], oh1[:, :, :], oh2[:, :, :], ALU.add)

        @block.scalar
        def _(act):
            act.wait_ge(diff_ready, 1)
            act.activation(e2[:, :], e2[:, :], ACT.Exp).then_inc(exp_ready, 1)


def moe0_bias(g, share):
    nc = g.nc
    with Stage(nc) as s:
        def fill(dve, dst, t):
            return dve.tensor_copy(dst[:, 0:NE], tile_at(share, t))

        def finish(dve, u, t, i, first, ps):
            return dve.tensor_tensor(tile_at(g.X, t), tile_at(g.X, t), ps, ALU.add)

        w = s.enter_context(nc.sbuf_tensor("mb_w", [NE, 1, D], F32))
        NodeStage(g, "mb", s, 1, D, [], None, fill=fill, finish=finish, finisher="dve", width=NE, w=w,
                  extra=[(w[:, 0, :], g.inp["L0_ffn_b2"])])


def moe0(g, share):
    nc = g.nc
    TG = G * P
    HB = TG // 2
    HC = F0 // P
    M = 2 * HC
    with Stage(nc) as s:
        rows_in, hid_done, gelu_done, out_done, added, copied, small, chain, pos_ready, lanes_ready = sems(
            nc, s, "m0", "rows_in hid_done gelu_done out_done added copied small chain pos_ready lanes_ready")
        assert 2 * NE * G == 2 * PLACES
        w_in = [s.semaphore(f"m0_w{e}") for e in range(NE)]
        landed = sems(nc, s, "m0", "landed0 landed1")
        sb = lambda n, sh, d=F32: s.enter_context(nc.sbuf_tensor("m0_" + n, sh, d))
        w1, w2 = sb("w1", [P, NE, KD, F0]), sb("w2", [P, NE, HC, D])
        b1 = sb("b1", [P, NE, HC])
        xg = sb("xg", [P, KD, TG])
        hid = sb("hid", [P, 2, HC, TG])
        ring = sb("ring", [EP, 2, SC, 3], I32)
        oh, cum, pos = sb("oh", [EP, EC], I32), sb("cum", [EP, EC]), sb("pos", [EP, EC])
        ps = s.enter_context(nc.psum_tensor("m0_ps", [P, 8, 512], F32))
        block = s.enter_context(nc.Block())

        @block.sync
        def _(sp):
            sp.dma_start(b1[:, :, :], g.inp["L0_ffn_b1"].rearrange("e (k p) -> p e k", p=P)).then_inc(small, 16)
            groups = g.xt.rearrange("p k (i c) -> p i k c", c=TG)

            def load(i, first):
                if not first:
                    sp.wait_ge(hid_done, NE * M * i)
                sp.dma_start(xg[:, :, :], groups[:, bass.ds(i, 1), :, :].rearrange("p a k c -> p (a k) c")).then_inc(rows_in, 16)
            load(0, True)
            for e in range(NE):
                sp.dma_start(w1[:, e], g.inp["L0_ffn_W1"][e].rearrange("(k p) c -> p k c", p=P)).then_inc(w_in[e], 16)
                sp.dma_start(w2[:, e], g.inp["L0_ffn_W2"][e].rearrange("(k p) c -> p k c", p=P)).then_inc(w_in[e], 16)
            with sp.Fori(1, NG) as i:
                load(i, False)

        @block.gpsimd
        def _(pool):
            pool.wait_ge(pos_ready, 1)
            scatter_pool(g, pool, 1, g.recs1, ring, copied, landed)

        @block.tensor
        def _(pe):
            def hidden(i, first, e):
                if first:
                    pe.wait_ge(w_in[e], 32)
                for m in range(M):
                    q = (NE * i + e) * M + m
                    if not first or e or m >= 4:
                        pe.wait_ge(gelu_done, q - 3)
                    hc, half = m // 2, m % 2
                    for k in range(KD):
                        ins = nc.tensor.matmul(ps[:, m % 4, 0:HB], w1[:, e, k, hc * P:(hc + 1) * P],
                                               xg[:, k, half * HB:(half + 1) * HB], start=k == 0, stop=k == KD - 1)
                    ins.then_inc(hid_done, 1)

            def outputs(i, first, e):
                pe.wait_ge(gelu_done, (NE * i + e + 1) * M)
                for u in range(G):
                    r = (NE * i + e) * G + u
                    if not first or e * G + u >= 4:
                        pe.wait_ge(added, r - 3)
                    bank = 4 + (e * G + u) % 4
                    for k in range(HC):
                        ins = nc.tensor.matmul(ps[:, bank, 0:D], hid[:, e % 2, k, u * P:(u + 1) * P],
                                               w2[:, e, k, :], start=k == 0, stop=k == HC - 1)
                    ins.then_inc(out_done, 1)

            def body(i, first):
                pe.wait_ge(rows_in, 16 * (i + 1))
                hidden(i, first, 0)
                for e in range(NE):
                    if e + 1 < NE:
                        hidden(i, first, e + 1)
                    outputs(i, first, e)
            each(pe, body, NG)

        @block.scalar
        def _(act):
            act.wait_ge(small, 16)

            def body(i, first):
                for e in range(NE):
                    if not first or e >= 2:
                        act.wait_ge(out_done, (NE * i + e - 1) * G)
                    for m in range(M):
                        hc, half = m // 2, m % 2
                        act.wait_ge(hid_done, (NE * i + e) * M + m + 1)
                        act.activation(hid[:, e % 2, hc, half * HB:(half + 1) * HB], ps[:, m % 4, 0:HB], ACT.Gelu,
                                       bias=b1[:, e, hc:hc + 1]).then_inc(gelu_done, 1)
            each(act, body, NG)

        @block.vector
        def _(dve):
            dve.memset(pos[:, :], 0.0).then_inc(chain, 1)

            def add(i, first, e, u):
                r = (NE * i + e) * G + u
                if not first or e:
                    dve.wait_ge(added, r - G + 1)
                dve.wait_ge(out_done, r + 1)
                x = tile_at(g.X, G * i + u)
                dve.scalar_tensor_tensor(x, ps[:, 4 + (e * G + u) % 4, 0:D],
                                         tile_at(share, G * i + u)[:, e:e + 1], x,
                                         ALU.mult, ALU.add).then_inc(added, 1)

            def with_places(i, first):
                for q in range(NE * G):
                    add(i, first, q // G, q % G)
                    b = NE * G // 2 * i + q // 2
                    for m in ((0, 1), (2,))[q % 2]:
                        places_step(g, dve, chain, 3 * b + 1, m, b, g.recs1, g.base1, oh, cum, pos)
            each(dve, with_places, 2)
            places_end(dve, chain, 3 * PLACES + 1, g.recs1, pos, oh, cum.bitcast(I32), pos_ready)

            def body(i):
                for q in range(NE * G):
                    add(i, False, q // G, q % G)
            with dve.Fori(2, NG) as i:
                body(i)


def gnn_rows(g):
    with Stage(g.nc) as s:
        bias = s.enter_context(g.nc.sbuf_tensor("gi_bias", [P, D], F32))

        def finish(dve, u, t, i, first, ps):
            return dve.tensor_tensor(tile_at(g.H, t), ps, bias[:, :], ALU.add)

        NodeStage(g, "gi", s, KD, D, [(0, KD, g.inp["L1_gnn_W_in"])], None, ln=1, finish=finish,
                  finisher="dve", store=StoreTile(g), extra=[(bias[:, :], every_partition(g.inp["L1_gnn_b_in"]))])


def every_partition(v):
    return v.rearrange("(a c) -> a c", a=1).broadcast_to([P, v.shape[0]])


class StoreTile:
    dmas = 1

    def __init__(self, g):
        self.g = g

    def __call__(self, sp, u, t, sem):
        sp.dma_start(tile_at(tiles_of(self.g.table), t), tile_at(self.g.H, t)).then_inc(sem, 16)


def gnn_sum(g, layer, acc):
    nc = g.nc
    W = D + 1
    with Stage(nc) as s:
        oh_ready, product, added, ready, one, loaded, h_ready, h_turned, ht_ready, h_product, h_kept = sems(
            nc, s, f"g{layer}", "oh_ready product added ready one loaded h_ready h_turned ht_ready h_product h_kept")
        assert C // STEP >= NT
        sb = lambda n, sh, d=F32: s.enter_context(nc.sbuf_tensor(f"g{layer}_" + n, sh, d))
        rows = sb("rows", [P, R, U, W])
        oh = sb("oh", [P, R, U, P])
        ps = s.enter_context(nc.psum_tensor(f"g{layer}_ps", [P, 8, 512], F32))
        w, b, ht = sb("w", [P, KD, D]), sb("b", [1, D]), sb("ht", [P, KD, P])
        hrow = sb("hrow", [P, D])
        HT, HW = 4, 5
        edges = EdgeRing(g, f"g{layer}e", s, g.rec[1], g.table, rows)
        block = s.enter_context(nc.Block())

        @block.sync
        def _(sp):
            sp.dma_start(w[:, :, :], g.inp["L1_gnn_W_self"][layer].rearrange("(k p) c -> p k c", p=P)).then_inc(loaded, 16)
            sp.dma_start(b[:, :], g.inp["L1_gnn_b_hid"][layer:layer + 1, :]).then_inc(loaded, 16)

        def rounds(engine, body):
            body(0, True, True)
            with engine.Fori(1, NT) as i:
                body(i, False, True)
            with engine.Fori(NT, C // STEP) as i:
                body(i, False, False)

        @block.gpsimd
        def _(pool):
            edges.gathers(pool, (product, U))

        @block.scalar
        def _(act):
            def body(i, first):
                for h in range(R):
                    edges.indices(act, i, h, first)
            each(act, body, C // STEP)

        @block.tensor
        def _(pe):
            pe.wait_ge(one, 1)
            pe.wait_ge(loaded, 32)

            def body(i, first, own):
                for h in range(R):
                    n = R * i + h
                    if own and h == 1:
                        pe.wait_ge(h_ready, i + 1)
                        for k in range(KD):
                            ins = nc.tensor.transpose(ps[:, HT, k * P:(k + 1) * P], hrow[:, k * P:(k + 1) * P], g.ident[:, :])
                        ins.then_inc(h_turned, 1)
                    if own and h == 3:
                        pe.wait_ge(ht_ready, i + 1)
                        if not first:
                            pe.wait_ge(h_kept, i)
                        for k in range(KD):
                            nc.tensor.matmul(ps[:, HW, 0:D], ht[:, k, :], w[:, k, :], start=k == 0, stop=False)
                        nc.tensor.matmul(ps[:, HW, 0:D], g.ones[0:1, :], b[:, :], start=False, stop=True).then_inc(h_product, 1)
                    edges.arrived(pe, i, h)
                    for k in range(U):
                        pe.wait_ge(oh_ready, U * n + k + 1)
                        if not (first and h == 0):
                            pe.wait_ge(added, (n - 1) * U + k + 1)
                        nc.tensor.matmul(ps[:, k, 0:W], oh[:, h, k, :], rows[:, h, k, :],
                                         start=True, stop=True).then_inc(product, 1)
            rounds(pe, body)

        @block.vector
        def _(dve):
            regs = tile_registers(dve, g, f"g{layer}_tile")
            dve.memset(rows[:, :, :, D:W], 1.0).then_inc(one, 1)
            dve.memset(acc[:, :, :], 0.0).then_inc(ready, 1)
            dve.wait_ge(ready, 1)

            def own_tile(i, h):
                if h == 0:
                    dve.tensor_copy(hrow[:, :], tile_at(g.H, i)).then_inc(h_ready, 1)
                if h == 2:
                    dve.wait_ge(h_turned, i + 1)
                    dve.tensor_copy(ht[:, :, :], ps[:, HT, 0:D].rearrange("p (k c) -> p k c", k=KD)).then_inc(ht_ready, 1)
                if h == 3:
                    dve.wait_ge(h_product, i + 1)
                    dve.sem_inc(g.settled, 1)
                    dve.tensor_copy(tile_at(g.H, i), ps[:, HW, 0:D]).then_inc(h_kept, 1)

            def step(n, h, known):
                def one_hot(k):
                    if known(0):
                        dve.tensor_scalar(oh[:, h, k, :], g.iota[:, :], g.rec[1][:, bass.ds(n * U + k, 1), 1], None,
                                          ALU.is_equal).then_inc(oh_ready, 1)

                def add_sum(k):
                    if known(1):
                        dve.wait_ge(product, (n - 1) * U + k + 1)
                        if known(2) or k:
                            dve.wait_ge(added, (n - 1) * U + k)
                        a = tile_at(acc, ts[k])
                        dve.tensor_tensor(a, a, ps[:, k, 0:W], ALU.add).then_inc(added, 1)

                if known(0) and known(R):
                    dve.wait_ge(product, (n - R + 1) * U)
                one_hot(0)
                one_hot(1)
                if known(1):
                    ts = load_tiles(dve, regs, g.tile_of[1], n - 1)
                add_sum(0)
                one_hot(2)
                add_sum(1)
                one_hot(3)
                add_sum(2)
                add_sum(3)

            def body(i, first, own):
                for h in range(R):
                    step(R * i + h, h, lambda b: h >= b or not first)
                    if own:
                        own_tile(i, h)
            rounds(dve, body)
            step(C // U, 0, lambda b: b > 0)


def gnn_update(g, layer, acc):
    nc = g.nc
    with Stage(nc) as s:
        inv = s.enter_context(nc.sbuf_tensor(f"gu{layer}_inv", [P, NT, 1], F32))
        step, = sems(nc, s, f"gu{layer}", "step")

        def setup_dve(dve, w, ready):
            dve.tensor_scalar(inv[:, :, :], acc[:, :, D:D + 1], 1.0, None, ALU.max).then_inc(step, 1)
            dve.wait_ge(step, 1)
            dve.reciprocal(inv[:, :, :], inv[:, :, :]).then_inc(step, 1)
            dve.wait_ge(step, 2)
            dve.sem_inc(ready, 1)

        def fill(dve, dst, t):
            return dve.tensor_scalar(dst, tile_at(acc, t)[:, 0:D], tile_at(inv, t), None, ALU.mult)

        def finish(dve, u, t, i, first, ps):
            return dve.tensor_tensor(tile_at(g.H, t), tile_at(g.H, t), ps, ALU.add)

        def last(act, t):
            return act.activation(tile_at(g.H, t), tile_at(g.H, t), ACT.Relu)

        NodeStage(g, f"gu{layer}", s, KD, D, [(0, KD, g.inp["L1_gnn_W_agg"][layer])], None, fill=fill,
                  finish=finish, finisher="dve", last=last, setup_dve=setup_dve,
                  store=StoreTile(g) if layer < 2 else None)


def gnn_out(g):
    with Stage(g.nc) as s:
        bias = s.enter_context(g.nc.sbuf_tensor("go_bias", [P, D], F32))

        def fill(dve, dst, t):
            dve.tensor_tensor(tile_at(g.X, t), tile_at(g.X, t), bias[:, :], ALU.add)
            return dve.tensor_copy(dst, tile_at(g.H, t))

        def finish(dve, u, t, i, first, ps):
            return dve.tensor_tensor(tile_at(g.X, t), tile_at(g.X, t), ps, ALU.add)

        NodeStage(g, "go", s, KD, D, [(0, KD, g.inp["L1_gnn_W_out"])], None, fill=fill, finish=finish,
                  finisher="dve", extra=[(bias[:, :], every_partition(g.inp["L1_gnn_b_out"]))])


def moe1_rows(g, xn, logits):
    with Stage(g.nc) as s:
        def keep(dve, rows, i):
            dve.tensor_copy(xn[:, bass.ds(G * i, G), :], rows[:, :, :])

        def finish(dve, u, t, i, first, ps):
            return dve.tensor_copy(tile_at(logits, t), ps)

        NodeStage(g, "nr", s, KD, NE, [(0, KD, g.inp["L1_ffn_gate_w"])], None, ln=1, keep=keep,
                  finish=finish, finisher="dve")


def moe1_pick(g, logits, prob, put, get):
    nc = g.nc
    with Stage(nc) as s:
        steps, arg_ready, exp_ready, oh_ready, counted, past_ready, loaded = sems(
            nc, s, "np", "steps arg_ready exp_ready oh_ready counted past_ready loaded")
        v = Small(nc, s, "np", steps)
        less8, tmp, oh, ex, tot, carry = v.new([P, NE]), *(v.new([P, NT, NE]) for _ in range(5))
        best, mx, rank, kept, e0, place = (v.new([P, NT]) for _ in range(6))
        past, bias = v.new([P, NT]), v.new([P, 1, NE])
        ps = s.enter_context(nc.psum_tensor("np_ps", [P, 2, 512], F32))
        block = s.enter_context(nc.Block())
        L = NT * NE

        @block.sync
        def _(sp):
            sp.dma_start(bias[:, 0, :], every_partition(g.inp["L1_ffn_gate_b"])).then_inc(loaded, 16)

        @block.gpsimd
        def _(pool):
            pool.iota(past[:, :], [[P, NT]], base=NE * SLOTS, channel_multiplier=1,
                      allow_small_or_imprecise_dtypes=True).then_inc(past_ready, 1)

        @block.tensor
        def _(pe):
            pe.wait_ge(oh_ready, 1)
            flat = oh[:, :, :].rearrange("p t e -> p (t e)")
            nc.tensor.matmul(ps[:, 0, 0:L], g.upto[:, :], flat, start=True, stop=True)
            nc.tensor.matmul(ps[:, 1, 0:L], g.ones[:, :], flat, start=True, stop=True).then_inc(counted, 1)

        @block.scalar
        def _(act):
            act.wait_ge(arg_ready, 1)
            act.activation(ex[:, :, :], tmp[:, :, :], ACT.Exp).then_inc(exp_ready, 1)

        @block.vector
        def _(dve):
            def go(ins):
                v.link(dve, ins)
            dve.wait_ge(loaded, 16)
            go(dve.tensor_tensor(logits[:, :, :], logits[:, :, :], bias[:, :, :].broadcast_to([P, NT, NE]), ALU.add))
            go(dve.tensor_scalar(less8[:, :], g.iota[:, 0:NE], float(NE), None, ALU.subtract))
            first_max(dve, v, logits, less8, tmp, best, oh, mx)
            dve.sem_inc(oh_ready, 1)
            dve.tensor_tensor(tmp[:, :, :], logits[:, :, :], mx[:, :].unsqueeze(2).broadcast_to([P, NT, NE]),
                              ALU.subtract).then_inc(arg_ready, 1)
            dve.wait_ge(exp_ready, 1)
            go(dve.tensor_reduce(prob[:, :], ex[:, :, :], AX.X, ALU.add))
            go(dve.reciprocal(prob[:, :], prob[:, :]))
            dve.wait_ge(counted, 1)
            go(dve.tensor_copy(tot[:, :, :], ps[:, 1, 0:L].rearrange("p (t e) -> p t e", e=NE)))
            for e in range(NE):
                ins = dve.tensor_tensor_scan(carry[:, :, e], tot[:, :, e], tot[:, :, e], 0.0, ALU.add, ALU.max)
            go(ins)
            go(dve.tensor_tensor(carry[:, :, :], carry[:, :, :], tot[:, :, :], ALU.subtract))
            go(dve.tensor_tensor(carry[:, :, :], carry[:, :, :], ps[:, 0, 0:L].rearrange("p (t e) -> p t e", e=NE), ALU.add))
            go(dve.tensor_tensor(carry[:, :, :], carry[:, :, :], oh[:, :, :], ALU.mult))
            go(dve.tensor_reduce(rank[:, :], carry[:, :, :], AX.X, ALU.add))
            go(dve.tensor_scalar(rank[:, :], rank[:, :], 1.0, None, ALU.subtract))
            go(dve.tensor_scalar(kept[:, :], rank[:, :], float(CAP), None, ALU.is_lt))
            go(dve.tensor_tensor(prob[:, :], prob[:, :], kept[:, :], ALU.mult))
            go(dve.tensor_scalar(e0[:, :], best[:, :], float(NE), float(SLOTS), ALU.add, ALU.mult))
            go(dve.scalar_tensor_tensor(place[:, :], rank[:, :], float(CAP - 1), e0[:, :], ALU.min, ALU.add))
            dve.tensor_copy(get[:, :], place[:, :])
            dve.wait_ge(past_ready, 1)
            go(dve.tensor_tensor(place[:, :], place[:, :], past[:, :], ALU.subtract))
            go(dve.tensor_tensor(place[:, :], place[:, :], kept[:, :], ALU.mult))
            go(dve.tensor_tensor(place[:, :], place[:, :], past[:, :], ALU.add))
            dve.tensor_copy(put[:, :], place[:, :])


def moe1_send(g, xn, put):
    nc = g.nc
    with Stage(nc) as s:
        sent, = sems(nc, s, "ns", "sent")
        block = s.enter_context(nc.Block())

        @block.gpsimd
        def _(pool):
            for t in range(NT):
                n = P if t < NT - 1 else LAST
                pool.indirect_dma_start(g.slots, bass.IndirectOffsetOnAxis(put[0:n, t:t + 1], 0),
                                        xn[0:n, t, :], None).then_inc(sent, 16)
            pool.wait_ge(sent, 16 * NT)


def moe1(g):
    nc = g.nc
    FC = F1 // P
    HALVES = ((0, 512), (512, CAP - 512))
    HP = len(HALVES) * FC
    with Stage(nc) as s:
        loaded = sems(nc, s, "n1", "loaded0 loaded1")
        stored = sems(nc, s, "n1", "stored0 stored1")
        small, turned, xt_ready, hid_done, relu_done, out_done, out_kept, y_zero = sems(
            nc, s, "n1", "small turned xt_ready hid_done relu_done out_done out_kept y_zero")
        sb = lambda n, sh, d=F32: s.enter_context(nc.sbuf_tensor("n1_" + n, sh, d))
        w1, w2 = sb("w1", [P, 2, KD, F1]), sb("w2", [P, 2, FC, D])
        rows = sb("rows", [P, 2, ST, D])
        xt = sb("xt", [P, KD, SLOTS])
        hid = sb("hid", [P, FC, SLOTS])
        y = sb("y", [P, 2, ST, D])
        b1, b2 = sb("b1", [P, NE, FC]), sb("b2", [1, NE, D])
        ps = s.enter_context(nc.psum_tensor("n1_ps", [P, 8, 512], F32))
        slots = g.slots[0:NE * SLOTS, :].rearrange("(e t p) d -> p e t d", p=P, t=ST)
        results = g.results.rearrange("(e t p) d -> p e t d", p=P, t=ST)
        block = s.enter_context(nc.Block())
        rows_of = lambda st: P if st < ST - 1 else CAP - (ST - 1) * P

        def tile_b2(e):
            return b2[:, bass.ds(e, 1), :].rearrange("p a c -> p (a c)")

        def pairs(engine, body):
            def both(i, first):
                for e2 in range(2):
                    body(i, e2, first)
            each(engine, both, NE // 2)

        @block.sync
        def _(sp):
            sp.dma_start(b1[:, :, :], g.inp["L1_ffn_b1"].rearrange("e (k p) -> p e k", p=P)).then_inc(small, 16)
            sp.dma_start(b2[:, :, :], g.inp["L1_ffn_b2"].rearrange("(a e) d -> a e d", a=1)).then_inc(small, 16)
            w1v = g.inp["L1_ffn_w1"].rearrange("e (k p) c -> p e k c", p=P)
            w2v = g.inp["L1_ffn_w2"].rearrange("e (k p) c -> p e k c", p=P)

            def body(i, e2, first):
                e = 2 * i + e2
                if not first:
                    sp.wait_ge(out_done, (e - 1) * ST)
                for dst, src in ((rows[:, e2], slots), (w1[:, e2], w1v), (w2[:, e2], w2v)):
                    sp.dma_start(dst, src[:, bass.ds(e, 1)].rearrange("p a k c -> p (a k) c")).then_inc(loaded[e2], 16)
            pairs(sp, body)

        @block.gpsimd
        def _(pool):
            def body(i, e2, first):
                e = 2 * i + e2
                pool.wait_ge(out_kept, (e + 1) * ST)
                pool.dma_start(results[:, bass.ds(e, 1)].rearrange("p a k c -> p (a k) c"), y[:, e2]).then_inc(stored[e2], 16)
            pairs(pool, body)
            for e2 in range(2):
                pool.wait_ge(stored[e2], 16 * NE // 2)

        @block.tensor
        def _(pe):
            pe.wait_ge(small, 32)

            def body(i, e2, first):
                e = 2 * i + e2
                pe.wait_ge(loaded[e2], 48 * (i + 1))
                for st in range(ST):
                    if not (first and e2 == 0 and st < 4):
                        pe.wait_ge(xt_ready, e * ST + st - 3)
                    if st == 0 and not (first and e2 == 0):
                        pe.wait_ge(relu_done, e * HP)
                    for k in range(KD):
                        ins = nc.tensor.transpose(ps[:, st % 4, k * P:(k + 1) * P], rows[:, e2, st, k * P:(k + 1) * P], g.ident[:, :])
                    ins.then_inc(turned, 1)
                pe.wait_ge(xt_ready, (e + 1) * ST)
                for m in range(HP):
                    q = e * HP + m
                    fc, (c0, cn) = m // 2, HALVES[m % 2]
                    if m >= 4:
                        pe.wait_ge(relu_done, q - 3)
                    for k in range(KD):
                        ins = nc.tensor.matmul(ps[:, m % 4, 0:cn], w1[:, e2, k, fc * P:(fc + 1) * P],
                                               xt[:, k, c0:c0 + cn], start=k == 0, stop=k == KD - 1)
                    ins.then_inc(hid_done, 1)
                pe.wait_ge(relu_done, (e + 1) * HP)
                for st in range(ST):
                    n = rows_of(st)
                    if not (first and e2 == 0 and st < 4):
                        pe.wait_ge(out_kept, e * ST + st - 3)
                    for k in range(FC):
                        nc.tensor.matmul(ps[0:n, 4 + st % 4, 0:D], hid[:, k, st * P:st * P + n], w2[:, e2, k, :],
                                         start=k == 0, stop=False)
                    nc.tensor.matmul(ps[0:n, 4 + st % 4, 0:D], g.ones[0:1, 0:n], tile_b2(e), start=False,
                                     stop=True).then_inc(out_done, 1)
            pairs(pe, body)

        @block.scalar
        def _(act):
            act.wait_ge(small, 32)

            def body(i, e2, first):
                e = 2 * i + e2
                for m in range(HP):
                    fc, (c0, cn) = m // 2, HALVES[m % 2]
                    act.wait_ge(hid_done, e * HP + m + 1)
                    if m == 0 and not (first and e2 == 0):
                        act.wait_ge(out_done, e * ST)
                    act.sem_inc(g.settled, 1)
                    act.activation(hid[:, fc, c0:c0 + cn], ps[:, m % 4, 0:cn], ACT.Relu,
                                   bias=b1[:, bass.ds(e, 1), fc:fc + 1].rearrange("p a c -> p (a c)")).then_inc(relu_done, 1)
            pairs(act, body)

        @block.vector
        def _(dve):
            def body(i, e2, first):
                e = 2 * i + e2
                for st in range(ST):
                    dve.wait_ge(turned, e * ST + st + 1)
                    if st == 0 and not (first and e2 == 0):
                        dve.wait_ge(hid_done, e * HP)
                    dve.tensor_copy(xt[:, :, st * P:(st + 1) * P],
                                    ps[:, st % 4, 0:D].rearrange("p (k c) -> p k c", k=KD)).then_inc(xt_ready, 1)
                if not first:
                    dve.wait_ge(stored[e2], 16 * i)
                for st in range(ST):
                    n = rows_of(st)
                    dve.wait_ge(out_done, e * ST + st + 1)
                    dve.tensor_copy(y[0:n, e2, st, :], ps[0:n, 4 + st % 4, 0:D]).then_inc(out_kept, 1)
            dve.memset(y[:, :, ST - 1, :], 0.0).then_inc(y_zero, 1)
            dve.wait_ge(y_zero, 1)
            pairs(dve, body)


def moe1_add(g, prob, get):
    nc = g.nc
    FMAX = 3.4028234e38
    INF = 1e4
    with Stage(nc) as s:
        scaled, chain, signed, alt_ready, taken, added, stored = sems(
            nc, s, "na", "scaled chain signed alt_ready taken added stored")
        landed = sems(nc, s, "na", "landed0 landed1")
        sb = lambda n, sh, d=F32: s.enter_context(nc.sbuf_tensor("na_" + n, sh, d))
        got, y = sb("got", [P, 2, G, D]), sb("y", [P, 2, G, D])
        sign, alt, fin = sb("sign", [P, G, D]), sb("alt", [P, G, D]), sb("fin", [P, G, D], I32)
        block = s.enter_context(nc.Block())

        @block.gpsimd
        def _(pool):
            for i in range(NG):
                if i >= 2:
                    pool.wait_ge(scaled, G * (i - 1))
                for u in range(G):
                    t = G * i + u
                    pool.indirect_dma_start(got[:, i % 2, u, :], None, g.results,
                                            bass.IndirectOffsetOnAxis(get[:, t:t + 1], 0)).then_inc(landed[i % 2], 16)

        @block.scalar
        def _(act):
            for i in range(NG):
                act.wait_ge(landed[i % 2], 16 * G * (i // 2 + 1))
                if i >= 2:
                    act.wait_ge(taken, i - 1)
                for u in range(G):
                    t = G * i + u
                    act.activation(y[:, i % 2, u, :], got[:, i % 2, u, :], ACT.Copy, scale=prob[:, t:t + 1]).then_inc(scaled, 1)
                act.wait_ge(signed, i + 1)
                if i:
                    act.wait_ge(added, i)
                act.activation(alt[:, :, :], sign[:, :, :], ACT.Copy, scale=-INF).then_inc(alt_ready, 1)

        @block.vector
        def _(dve):
            for i in range(NG):
                yi = y[:, i % 2]
                x = g.X[:, G * i:G * (i + 1), :]
                dve.wait_ge(scaled, G * (i + 1))
                if i:
                    dve.wait_ge(alt_ready, i)
                dve.tensor_scalar(sign[:, :, :], yi, FMAX, None, ALU.is_gt).then_inc(chain, 1)
                dve.tensor_scalar(fin[:, :, :], yi, 0.0, 0.0, ALU.mult, ALU.is_equal)
                dve.wait_ge(chain, i + 1)
                dve.scalar_tensor_tensor(sign[:, :, :], yi, -FMAX, sign[:, :, :], ALU.is_lt, ALU.subtract).then_inc(signed, 1)
                dve.wait_ge(alt_ready, i + 1)
                dve.copy_predicated(alt[:, :, :], fin[:, :, :], yi).then_inc(taken, 1)
                dve.wait_ge(taken, i + 1)
                dve.tensor_tensor(x, x, alt[:, :, :], ALU.add).then_inc(added, 1)

        @block.sync
        def _(sp):
            for i in range(NG):
                sp.wait_ge(added, i + 1)
                full = G if i < NG - 1 else G - 1
                r0 = G * i * P
                sp.dma_start(g.out[r0:r0 + full * P, :].rearrange("(t p) d -> p t d", p=P), g.X[:, G * i:G * i + full, :]).then_inc(stored, 16)
            sp.dma_start(g.out[(NT - 1) * P:N, :], g.X[0:LAST, NT - 1, :]).then_inc(stored, 16)
            sp.wait_ge(stored, 16 * (NG + 1))


def kernel_body(nc, inputs, out):
    g = Ctx(nc, inputs, out)
    with ExitStack() as s:
        sb = lambda n, sh, d=F32: s.enter_context(nc.sbuf_tensor(n, sh, d))
        dr = lambda n, sh, d=F32: nc.dram_tensor(n, sh, d, kind="Internal").ap()
        s.enter_context(nc.allow_non_contiguous_dma("a few vectors of a few hundred elements, put on partitions"))
        g.settled = s.enter_context(nc.semaphore("settled"))
        g.X = sb("X", [P, NT, D])
        g.ones, g.ident, g.iota = sb("ones", [P, P]), sb("ident", [P, P]), sb("iota", [P, P])
        g.before, g.upto = sb("before", [P, P]), sb("upto", [P, P])
        g.wa = sb("wa", [P, KD, 2 * HEADS])
        g.tile_of = [sb(f"tile_of{i}", [1, C], I32) for i in range(2)]
        g.records = [dr(f"records{i}", (P, C, 2), I32) for i in range(2)]
        g.unsorted = sb("unsorted", [1, 1], I32)
        g.blocks = dr("blocks", (BLOCKS + 1, 2, P), I32)
        g.table, g.score_table = dr("table", (NP, D)), dr("score_table", (NP, HEADS))
        g.xt = dr("xt", (P, KD, NP))
        g.slots, g.results = dr("slots", (NE * SLOTS + NP, D)), dr("results", (NE * SLOTS, D))
        alloc = lambda stack, n, sh, d=F32: stack.enter_context(nc.sbuf_tensor(n, sh, d))
        with ExitStack() as s2:
            g.recs1 = alloc(s2, "recs1", [EP, EC, 3], I32)
            g.base1 = alloc(s2, "base1", [EP, PLACES])
            with ExitStack() as s3:
                g.rec = [alloc(s3, "rec0", [P, C, 2], I32)]
                setup(g)
                edge_blocks(g)
                bucket(g, 0)
                bucket(g, 1)
                halves = alloc(s3, "halves", [P, NT, 2 * HEADS])
                scores = alloc(s3, "scores", [P, C, HEADS])
                self_arg = alloc(s3, "self_arg", [P, NT, HEADS])
                own = alloc(s3, "own", [P, NT, 2 * HEADS])
                att_weights(g)
                gat_rows(g, halves)
                gat_max(g, halves, scores, own, self_arg)
                acc = alloc(s3, "gat_acc", [P, NT, D + HEADS])
                gat_sum(g, scores, own, self_arg, acc)
                gat_finish(g, acc)
            logits, share = alloc(s2, "logits0", [P, NT, NE]), alloc(s2, "share", [P, NT, NE])
            moe0_rows(g, logits)
            moe0_pick(g, logits, share)
            moe0_bias(g, share)
            moe0(g, share)
        with ExitStack() as s2:
            g.rec = [None, alloc(s2, "rec1", [P, C, 2], I32)]
            g.H = alloc(s2, "H", [P, NT, D])
            fetch(g, 1)
            gnn_rows(g)
            for layer in range(3):
                with ExitStack() as s3:
                    acc = alloc(s3, f"acc{layer}", [P, NT, D + 1])
                    gnn_sum(g, layer, acc)
                    gnn_update(g, layer, acc)
            gnn_out(g)
        with ExitStack() as s2:
            prob = alloc(s2, "prob", [P, NT])
            put, get = alloc(s2, "put", [P, NT], U32), alloc(s2, "get", [P, NT], U32)
            with ExitStack() as s3:
                xn, logits = alloc(s3, "xn", [P, NT, D]), alloc(s3, "logits1", [P, NT, NE])
                moe1_rows(g, xn, logits)
                moe1_pick(g, logits, prob, put, get)
                moe1_send(g, xn, put)
            moe1(g)
            moe1_add(g, prob, get)


def fetch(g, which):
    nc = g.nc
    with Stage(g.nc) as s:
        loaded, = sems(nc, s, f"fetch{which}", "loaded")
        block = s.enter_context(nc.Block())

        @block.sync
        def _(sp):
            sp.dma_start(g.rec[which][:, :, :], g.records[which]).then_inc(loaded, 16)
            sp.wait_ge(loaded, 16)


NAMES = ["x", "src", "dst", "L0_gnn_W", "L0_gnn_att_src", "L0_gnn_att_dst", "L0_gnn_bias", "L0_ffn_gamma",
         "L0_ffn_beta", "L0_ffn_Wr", "L0_ffn_br", "L0_ffn_W1", "L0_ffn_b1", "L0_ffn_W2", "L0_ffn_b2",
         "L1_gnn_W_in", "L1_gnn_b_in", "L1_gnn_W_agg", "L1_gnn_W_self", "L1_gnn_b_hid", "L1_gnn_W_out",
         "L1_gnn_b_out", "L1_ffn_gate_w", "L1_ffn_gate_b", "L1_ffn_w1", "L1_ffn_b1", "L1_ffn_w2", "L1_ffn_b2"]


def kernel(**inputs):
    import concourse.bacc as bacc
    from concourse.bass_utils import run_bass_kernel_spmd as run

    nc = bacc.Bacc("TRN2", target_bir_lowering=False, num_devices=1)
    arrays, aps = {}, {}
    for name in NAMES:
        a = np.ascontiguousarray(inputs[name])
        arrays[f"in_{name}"] = a
        aps[name] = nc.dram_tensor(f"in_{name}", a.shape, mybir.dt.from_np(a.dtype), kind="ExternalInput").ap()
    out = nc.dram_tensor("out", (N, D), F32, kind="ExternalOutput").ap()
    kernel_body(nc, aps, out)
    r = run(nc, [arrays], core_ids=[0])
    return r.results[0]["out"]
```
